# Optimizing a Trainium2 kernel written in Bass

```python
import numpy as np
import jax
import jax.numpy as jnp

def _softmax(x, axis=-1):
    return jax.nn.softmax(x, axis=axis)

def _gelu(x):
    return jax.nn.gelu(x, approximate=True)

def _silu(x):
    return jax.nn.silu(x)

def _sigmoid(x):
    return jax.nn.sigmoid(x)

def _layernorm(x, axis=-1, eps=1e-05):
    m = jnp.mean(x, axis=axis, keepdims=True)
    v = jnp.var(x, axis=axis, keepdims=True)
    return (x - m) / jnp.sqrt(v + eps)

def _scatter_add(tgt, idx, src, axis=0):
    return tgt.at[idx].add(src)

def _segment_sum(src, seg, n):
    return jax.ops.segment_sum(src, seg, n)
kernel_name = 'mk_gnn_resnorm_d4_gnn_r32_36c5e9'

def setup_inputs(seed: int=0):
    np.random.seed(seed)
    _w = jnp.asarray

    def _rec_inputs():
        import jax
        import jax.numpy as jnp
        _gk = jax.random.key(seed)
        x = -0.0004402 + 1 * jax.random.normal(jax.random.fold_in(_gk, 1), (3125, 16), jnp.float32)
        _s = jax.random.randint(jax.random.fold_in(_gk, 2), (50000,), 0, 3125, jnp.int32)
        _d = jax.random.randint(jax.random.fold_in(_gk, 3), (50000,), 0, 3125, jnp.int32)
        _loop = jnp.arange(3125, dtype=jnp.int32)
        src = jnp.concatenate([_s, _d, _loop])
        dst = jnp.concatenate([_d, _s, _loop])
        _o = jnp.argsort(dst, stable=True)
        src = src[_o]
        dst = dst[_o]
        edge_attr_16 = -3.57403e-05 + 0.999761 * jax.random.normal(jax.random.fold_in(_gk, 12), (103125, 16), jnp.float32)
        edge_attr_6 = jax.random.uniform(jax.random.fold_in(_gk, 13), (103125, 6), jnp.float32, 0.0, 1)
        return (x, src, dst, edge_attr_16, edge_attr_6)
    x, src, dst, edge_attr_16, edge_attr_6 = _rec_inputs()

    def _L0_gnn_setup():
        import jax, jax.numpy as jnp
        import numpy as np
        N_NODES = 30000
        N_EDGES = 9375
        IN_FEATS = 16
        OUT_FEATS = 16
        EDGE_DIM = 16
        key = jax.random.key(seed)
        ks = jax.random.split(key, 8)
        feat = jax.random.normal(ks[0], (N_NODES, IN_FEATS), dtype=jnp.float32)
        efeat = jax.random.normal(ks[1], (N_EDGES, EDGE_DIM), dtype=jnp.float32)
        W_msg = jax.random.normal(ks[2], (EDGE_DIM, IN_FEATS * OUT_FEATS), dtype=jnp.float32) * 0.1
        b_msg = jnp.zeros((IN_FEATS * OUT_FEATS,), dtype=jnp.float32)
        W_attn = jax.random.normal(ks[3], (EDGE_DIM, IN_FEATS * OUT_FEATS), dtype=jnp.float32) * 0.1
        b_attn = jnp.zeros((IN_FEATS * OUT_FEATS,), dtype=jnp.float32)
        src = jax.random.randint(ks[4], (N_EDGES,), 0, N_NODES, dtype=jnp.int32)
        dst = jax.random.randint(ks[5], (N_EDGES,), 0, N_NODES, dtype=jnp.int32)
        return {'feat': feat, 'efeat': efeat, 'W_msg': W_msg, 'b_msg': b_msg, 'W_attn': W_attn, 'b_attn': b_attn, 'src': src, 'dst': dst}
    _L0_gnn_all = _L0_gnn_setup()
    _L0_gnn_in = {k: v for k, v in _L0_gnn_all.items() if k in ('W_msg', 'b_msg', 'W_attn', 'b_attn')}
    del _L0_gnn_all

    def _L1_gnn_setup():
        import jax, jax.numpy as jnp
        import numpy as np
        LATENT = 16
        KDIM = 128
        EDIM = 6
        DEPTH = 4
        N_NODES = 50000
        N_EDGES = 25000

        def _kernel_net(edge_attr, kW1, kb1, kW2, kb2, kW3, kb3):
            h = jax.nn.gelu(edge_attr @ kW1 + kb1)
            h = jax.nn.gelu(h @ kW2 + kb2)
            return h @ kW3 + kb3
        key = jax.random.key(seed)
        ks = jax.random.split(key, 12)
        inp = {'nodes': jax.random.normal(ks[0], (N_NODES, LATENT), dtype=jnp.float32), 'edge_index': jax.random.randint(ks[1], (2, N_EDGES), 0, N_NODES, dtype=jnp.int64), 'edge_attr': jax.random.uniform(ks[2], (N_EDGES, EDIM), dtype=jnp.float32), 'kW1': jax.random.normal(ks[3], (EDIM, KDIM), dtype=jnp.float32) / np.sqrt(EDIM), 'kb1': jnp.zeros((KDIM,), dtype=jnp.float32), 'kW2': jax.random.normal(ks[4], (KDIM, KDIM), dtype=jnp.float32) / np.sqrt(KDIM), 'kb2': jnp.zeros((KDIM,), dtype=jnp.float32), 'kW3': jax.random.normal(ks[5], (KDIM, LATENT * LATENT), dtype=jnp.float32) / np.sqrt(KDIM), 'kb3': jnp.zeros((LATENT * LATENT,), dtype=jnp.float32), 'root_W': jax.random.normal(ks[6], (DEPTH, LATENT, LATENT), dtype=jnp.float32) / np.sqrt(LATENT), 'root_b': jnp.zeros((DEPTH, LATENT), dtype=jnp.float32)}
        return inp
    _L1_gnn_all = _L1_gnn_setup()
    _L1_gnn_in = {k: v for k, v in _L1_gnn_all.items() if k in ('kW1', 'kb1', 'kW2', 'kb2', 'kW3', 'kb3', 'root_W', 'root_b')}
    del _L1_gnn_all

    def _L2_gnn_setup():
        import jax, jax.numpy as jnp
        import numpy as np
        N_NODES = 6250
        N_EDGES = 100000
        F_IN = 16
        N_CLASSES = 16

        def _gin_conv(x, src, dst, eps, wa, ba, wb, bb, n_nodes):
            agg = jax.ops.segment_sum(x[src], dst, num_segments=n_nodes)
            h = (1.0 + eps) * x + agg
            h = jax.nn.relu(h @ wa + ba) @ wb + bb
            return h
        key = jax.random.key(seed)
        ks = jax.random.split(key, 8)
        s = 1.0 / np.sqrt(F_IN)
        return {'x': jax.random.normal(ks[0], (N_NODES, F_IN), dtype=jnp.float32), 'edge_index': jax.random.randint(ks[1], (2, N_EDGES), 0, N_NODES, dtype=jnp.int32), 'eps1': jnp.zeros((), dtype=jnp.float32), 'w1a': jax.random.normal(ks[2], (F_IN, 16), dtype=jnp.float32) * s, 'b1a': jnp.zeros((16,), dtype=jnp.float32), 'w1b': jax.random.normal(ks[3], (16, 16), dtype=jnp.float32) * 0.25, 'b1b': jnp.zeros((16,), dtype=jnp.float32), 'eps2': jnp.zeros((), dtype=jnp.float32), 'w2a': jax.random.normal(ks[4], (16, N_CLASSES), dtype=jnp.float32) * 0.25, 'b2a': jnp.zeros((N_CLASSES,), dtype=jnp.float32), 'w2b': jax.random.normal(ks[5], (N_CLASSES, N_CLASSES), dtype=jnp.float32) * 0.25, 'b2b': jnp.zeros((N_CLASSES,), dtype=jnp.float32)}
    _L2_gnn_all = _L2_gnn_setup()
    _L2_gnn_in = {k: v for k, v in _L2_gnn_all.items() if k in ('eps1', 'w1a', 'b1a', 'w1b', 'b1b', 'eps2', 'w2a', 'b2a', 'w2b', 'b2b')}
    del _L2_gnn_all

    def _L3_gnn_setup():
        import jax, jax.numpy as jnp
        import numpy as np
        N_NODES = 3125
        N_EDGES = 50000
        IN_DIM = 16
        OUT_DIM = 16
        E_DIM = 6
        EDGE_H = 64
        BN_EPS = 1e-05
        key = jax.random.key(seed)
        ks = jax.random.split(key, 8)
        h = jax.random.normal(ks[0], (N_NODES, IN_DIM), dtype=jnp.float32)
        efeat = jax.random.normal(ks[1], (N_EDGES, E_DIM), dtype=jnp.float32)
        src = jax.random.randint(ks[2], (N_EDGES,), 0, N_NODES, dtype=jnp.int32)
        dst = jax.random.randint(ks[3], (N_EDGES,), 0, N_NODES, dtype=jnp.int32)
        W1 = jax.random.normal(ks[4], (E_DIM, EDGE_H), dtype=jnp.float32) * 0.1
        b1 = jnp.zeros((EDGE_H,), dtype=jnp.float32)
        W2 = jax.random.normal(ks[5], (EDGE_H, IN_DIM * OUT_DIM), dtype=jnp.float32) * 0.1
        b2 = jnp.zeros((IN_DIM * OUT_DIM,), dtype=jnp.float32)
        bias = jnp.zeros((OUT_DIM,), dtype=jnp.float32)
        gamma = jnp.ones((OUT_DIM,), dtype=jnp.float32)
        beta = jnp.zeros((OUT_DIM,), dtype=jnp.float32)
        return {'h': h, 'efeat': efeat, 'src': src, 'dst': dst, 'W1': W1, 'b1': b1, 'W2': W2, 'b2': b2, 'bias': bias, 'gamma': gamma, 'beta': beta}
    _L3_gnn_all = _L3_gnn_setup()
    _L3_gnn_in = {k: v for k, v in _L3_gnn_all.items() if k in ('W1', 'b1', 'W2', 'b2', 'bias', 'gamma', 'beta')}
    del _L3_gnn_all
    return {'x': x, 'src': src, 'dst': dst, 'edge_attr_16': edge_attr_16, 'edge_attr_6': edge_attr_6, 'L0_gnn_W_msg': _L0_gnn_in['W_msg'], 'L0_gnn_b_msg': _L0_gnn_in['b_msg'], 'L0_gnn_W_attn': _L0_gnn_in['W_attn'], 'L0_gnn_b_attn': _L0_gnn_in['b_attn'], 'L1_gnn_kW1': _L1_gnn_in['kW1'], 'L1_gnn_kb1': _L1_gnn_in['kb1'], 'L1_gnn_kW2': _L1_gnn_in['kW2'], 'L1_gnn_kb2': _L1_gnn_in['kb2'], 'L1_gnn_kW3': _L1_gnn_in['kW3'], 'L1_gnn_kb3': _L1_gnn_in['kb3'], 'L1_gnn_root_W': _L1_gnn_in['root_W'], 'L1_gnn_root_b': _L1_gnn_in['root_b'], 'L2_gnn_eps1': _L2_gnn_in['eps1'], 'L2_gnn_w1a': _L2_gnn_in['w1a'], 'L2_gnn_b1a': _L2_gnn_in['b1a'], 'L2_gnn_w1b': _L2_gnn_in['w1b'], 'L2_gnn_b1b': _L2_gnn_in['b1b'], 'L2_gnn_eps2': _L2_gnn_in['eps2'], 'L2_gnn_w2a': _L2_gnn_in['w2a'], 'L2_gnn_b2a': _L2_gnn_in['b2a'], 'L2_gnn_w2b': _L2_gnn_in['w2b'], 'L2_gnn_b2b': _L2_gnn_in['b2b'], 'L3_gnn_W1': _L3_gnn_in['W1'], 'L3_gnn_b1': _L3_gnn_in['b1'], 'L3_gnn_W2': _L3_gnn_in['W2'], 'L3_gnn_b2': _L3_gnn_in['b2'], 'L3_gnn_bias': _L3_gnn_in['bias'], 'L3_gnn_gamma': _L3_gnn_in['gamma'], 'L3_gnn_beta': _L3_gnn_in['beta']}

def reference(x, src, dst, edge_attr_16, edge_attr_6, L0_gnn_W_msg, L0_gnn_b_msg, L0_gnn_W_attn, L0_gnn_b_attn, L1_gnn_kW1, L1_gnn_kb1, L1_gnn_kW2, L1_gnn_kb2, L1_gnn_kW3, L1_gnn_kb3, L1_gnn_root_W, L1_gnn_root_b, L2_gnn_eps1, L2_gnn_w1a, L2_gnn_b1a, L2_gnn_w1b, L2_gnn_b1b, L2_gnn_eps2, L2_gnn_w2a, L2_gnn_b2a, L2_gnn_w2b, L2_gnn_b2b, L3_gnn_W1, L3_gnn_b1, L3_gnn_W2, L3_gnn_b2, L3_gnn_bias, L3_gnn_gamma, L3_gnn_beta):
    import jax
    import jax.numpy as jnp

    def _L0_gnn_ref(feat, efeat, W_msg, b_msg, W_attn, b_attn, src, dst):
        import jax, jax.numpy as jnp
        import numpy as np
        N_NODES = 30000
        N_EDGES = 9375
        IN_FEATS = 16
        OUT_FEATS = 16
        EDGE_DIM = 16
        N, in_f = feat.shape
        E = efeat.shape[0]
        w_m = (efeat @ W_msg + b_msg).reshape(E, in_f, -1)
        w_a = (efeat @ W_attn + b_attn).reshape(E, in_f, -1)
        h_src = feat[src][:, :, None]
        e1 = w_m * h_src
        e2 = w_a * h_src
        seg_max = jax.ops.segment_max(e2, dst, num_segments=N)
        ex = jnp.exp(e2 - seg_max[dst])
        denom = jax.ops.segment_sum(ex, dst, num_segments=N)
        attn = ex / denom[dst]
        ft = jax.ops.segment_sum(e1 * attn, dst, num_segments=N)
        return ft.sum(axis=1)

    def _L1_gnn_ref(nodes, edge_attr, kW1, kb1, kW2, kb2, kW3, kb3, root_W, root_b, edge_index):
        import jax, jax.numpy as jnp
        import numpy as np
        LATENT = 16
        KDIM = 128
        EDIM = 6
        DEPTH = 4
        N_NODES = 50000
        N_EDGES = 25000

        def _kernel_net(edge_attr, kW1, kb1, kW2, kb2, kW3, kb3):
            h = jax.nn.gelu(edge_attr @ kW1 + kb1)
            h = jax.nn.gelu(h @ kW2 + kb2)
            return h @ kW3 + kb3
        src, dst = (edge_index[0], edge_index[1])
        n = nodes.shape[0]
        w = _kernel_net(edge_attr, kW1, kb1, kW2, kb2, kW3, kb3).reshape(-1, LATENT, LATENT)
        deg = jax.ops.segment_sum(jnp.ones((src.shape[0],), nodes.dtype), dst, num_segments=n)
        inv_deg = jnp.where(deg > 0, 1.0 / jnp.maximum(deg, 1.0), 0.0)[:, None]
        for i in range(DEPTH):
            msg = jnp.einsum('ei,eio->eo', nodes[src], w)
            agg = jax.ops.segment_sum(msg, dst, num_segments=n)
            agg = agg * inv_deg
            nodes = jax.nn.gelu(agg + nodes @ root_W[i] + root_b[i])
        return nodes

    def _L2_gnn_ref(x, edge_index, eps1, w1a, b1a, w1b, b1b, eps2, w2a, b2a, w2b, b2b):
        import jax, jax.numpy as jnp
        import numpy as np
        N_NODES = 6250
        N_EDGES = 100000
        F_IN = 16
        N_CLASSES = 16

        def _gin_conv(x, src, dst, eps, wa, ba, wb, bb, n_nodes):
            agg = jax.ops.segment_sum(x[src], dst, num_segments=n_nodes)
            h = (1.0 + eps) * x + agg
            h = jax.nn.relu(h @ wa + ba) @ wb + bb
            return h
        src, dst = (edge_index[0], edge_index[1])
        n = x.shape[0]
        h = jax.nn.relu(_gin_conv(x, src, dst, eps1, w1a, b1a, w1b, b1b, n))
        h = _gin_conv(h, src, dst, eps2, w2a, b2a, w2b, b2b, n)
        return jax.nn.log_softmax(h, axis=1)

    def _L3_gnn_ref(h, efeat, src, dst, W1, b1, W2, b2, bias, gamma, beta):
        import jax, jax.numpy as jnp
        import numpy as np
        N_NODES = 3125
        N_EDGES = 50000
        IN_DIM = 16
        OUT_DIM = 16
        E_DIM = 6
        EDGE_H = 64
        BN_EPS = 1e-05
        E = efeat.shape[0]
        N = h.shape[0]
        w = jax.nn.relu(efeat @ W1 + b1) @ W2 + b2
        w = w.reshape(E, IN_DIM, OUT_DIM)
        msg = jnp.einsum('ei,eio->eo', h[src], w)
        agg = jax.ops.segment_sum(msg, dst, num_segments=N)
        deg = jax.ops.segment_sum(jnp.ones((E,), h.dtype), dst, num_segments=N)
        out = agg / jnp.maximum(deg, 1.0)[:, None] + bias
        r = jax.nn.relu(out)
        mean = jnp.mean(r, axis=0)
        var = jnp.mean((r - mean) ** 2, axis=0)
        return (r - mean) * jax.lax.rsqrt(var + BN_EPS) * gamma + beta
    edge_index = jnp.stack([src, dst])
    x = _layernorm(x + _L0_gnn_ref(x, edge_attr_16, L0_gnn_W_msg, L0_gnn_b_msg, L0_gnn_W_attn, L0_gnn_b_attn, src, dst), axis=-1)
    x = _layernorm(x + _L1_gnn_ref(x, edge_attr_6, L1_gnn_kW1, L1_gnn_kb1, L1_gnn_kW2, L1_gnn_kb2, L1_gnn_kW3, L1_gnn_kb3, L1_gnn_root_W, L1_gnn_root_b, edge_index), axis=-1)
    x = _layernorm(x + _L2_gnn_ref(x, edge_index, L2_gnn_eps1, L2_gnn_w1a, L2_gnn_b1a, L2_gnn_w1b, L2_gnn_b1b, L2_gnn_eps2, L2_gnn_w2a, L2_gnn_b2a, L2_gnn_w2b, L2_gnn_b2b), axis=-1)
    x = _layernorm(x + _L3_gnn_ref(x, edge_attr_6, src, dst, L3_gnn_W1, L3_gnn_b1, L3_gnn_W2, L3_gnn_b2, L3_gnn_bias, L3_gnn_gamma, L3_gnn_beta), axis=-1)
    return x

_drawn_inputs = setup_inputs


def setup_inputs(seed=0):
    import zlib

    import numpy as np

    out = dict(_drawn_inputs(seed))
    spreads = {'L0_gnn_b_msg': (0.0, 0.1),
     'L0_gnn_b_attn': (0.0, 0.1),
     'L1_gnn_kb1': (0.0, 0.1),
     'L1_gnn_kb2': (0.0, 0.1),
     'L1_gnn_kb3': (0.0, 0.1),
     'L1_gnn_root_b': (0.0, 0.1),
     'L2_gnn_b1a': (0.0, 0.761),
     'L2_gnn_b1b': (0.0, 0.548),
     'L2_gnn_b2a': (0.0, 2.0),
     'L2_gnn_b2b': (0.0, 0.8),
     'L3_gnn_b1': (0.0, 0.1),
     'L3_gnn_b2': (0.0, 0.1),
     'L3_gnn_bias': (0.0, 0.1),
     'L3_gnn_gamma': (1.0, 0.2),
     'L3_gnn_beta': (0.0, 0.1)}
    factors = {}
    for name, (base, spread) in spreads.items():
        noise = np.random.default_rng([zlib.crc32(name.encode()), seed]).standard_normal(out[name].shape)
        drawn = base * np.exp(spread * noise) if base else spread * noise
        out[name] = jnp.asarray(drawn.astype(out[name].dtype))
    for name, factor in factors.items():
        out[name] = (out[name] * factor).astype(out[name].dtype)
    return out
```

```python
import concourse.bass as bass
from concourse import mybir
from contextlib import ExitStack

N = 3125
E = 103125
F = 16
P = 128
HI = -(-N // P)
NF = HI * F
NPAD = HI * P
CH = 512
TPC = CH // P
C = 2 * (-(-E // (2 * CH)))
T = C * TPC
EP = C * CH
W = F * F
HALF = W // 2
KD = 128
EH = 64
D16, D6 = 16, 6
DEPTH = 4
LN_EPS = 1e-5
BN_EPS = 1e-5
NEG = -3.0e38
PHASES = 1 + DEPTH + 2 + 1
L0, L1, L2, L3 = 0, 1, 1 + DEPTH, 3 + DEPTH

W_ROOT, W_1A, W_1B, W_2A, W_2B, NWM = 0, 4, 5, 6, 7, 8
B_ROOT, B_1A, B_1B, B_2A, B_2B, B_BIAS, B_GAMMA, B_BETA, NBR = 0, 4, 5, 6, 7, 8, 9, 10, 11
K_ID, K_IOTA, K_SEL, K_VALID, NK = 0, P, 2 * P, 2 * P + F, 2 * P + F + HI


def pipeline(eng, stages, lead=2):
    for c in range(lead):
        for stage, lag in stages:
            if c >= lag:
                stage(c - lag, (c - lag) % 2, (c - lag) // 2)
    with eng.Fori(0, (C - lead) // 2) as i:
        for j in range(2):
            for stage, lag in stages:
                at = lead + j - lag
                stage(i * 2 + at, at % 2, i + at // 2)
    last = max(lag for _, lag in stages)
    for c in range(C, C + last):
        for stage, lag in stages:
            if c - lag < C:
                stage(c - lag, (c - lag) % 2, (c - lag) // 2)


def gnn_resnorm(nc, x, src_t, dst_t, dst_next_t, dst_row, dst_prev_row, ef16, ef6, w_attn, w_msg,
                kw1, kw2, kb2, kw3, kb3, l3w1, l3w2, node_w, node_b, eps, consts, out):
    f32, bf16, i32 = mybir.dt.float32, mybir.dt.bfloat16, mybir.dt.int32
    ALU, ACT, X = mybir.AluOpType, mybir.ActivationFunctionType, mybir.AxisListType.X
    v, s, g, te = nc.vector, nc.scalar, nc.gpsimd, nc.tensor

    tables = [x] + [nc.dram_tensor(f"node_table_{p}", (NPAD, F), f32, kind="Internal").ap()
                    for p in range(1, PHASES)]
    start_d = nc.dram_tensor("start_mask", (EP,), f32, kind="Internal").ap()
    h2_d = nc.dram_tensor("edge_hidden", (C, P, CH), f32, kind="Internal").ap()

    ctx = ExitStack()
    with ctx:
        def sb(name, shape, dt=f32):
            return ctx.enter_context(nc.sbuf_tensor(name, shape, dt))

        def sem(name):
            return ctx.enter_context(nc.semaphore(name))

        def sems(name, n):
            return [sem(f"{name}_{k}") for k in range(n)]

        src_sb = sb("src_sb", [P, T], i32)
        dlo = sb("dlo", [P, T])
        is_end = sb("is_end", [P, T])
        ohi = sb("ohi", [P, T, HI], bf16)
        con = sb("con", [P, NK])
        ident, iota = con[:, K_ID:K_ID + P], con[:, K_IOTA:K_IOTA + P]
        sel, valid = con[:, K_SEL:K_SEL + F], con[:, K_VALID:K_VALID + HI]
        nw = sb("nw", [P, NWM, P])
        nb = sb("nb", [P, NBR, F])
        eps_sb = sb("eps_sb", [P, 2])
        zer = sb("zer", [P, CH])
        ones = sb("ones", [P, P])
        wa_sb = sb("wa_sb", [D16 + 1, W])
        wm_sb = sb("wm_sb", [D16 + 1, W])
        kw1_sb = sb("kw1_sb", [D6 + 1, KD])
        kw2_sb = sb("kw2_sb", [P, KD])
        kb2_sb = sb("kb2_sb", [P, 1])
        kw3_sb = sb("kw3_sb", [P, W])
        l3w1_sb = sb("l3w1_sb", [D6 + 1, EH])
        l3w2_sb = sb("l3w2_sb", [EH + 1, W])
        kb3_rows = sb("kb3_rows", [P, W], bf16)
        ones_rows = sb("ones_rows", [P, P], bf16)
        xn = sb("xn", [P, CH])
        nodes = sb("nodes", [P, CH])
        zt_sb = sb("zt_sb", [P, CH])
        t1 = sb("t1", [P, CH])
        t2 = sb("t2", [P, CH])
        st = sb("st", [P, 6, HI])
        fs = sb("fs", [P, 4, F])
        inv_deg = sb("inv_deg", [P, HI])
        inv_deg1 = sb("inv_deg1", [P, HI])
        idx = sb("idx", [P, 2, TPC], i32)
        xg = sb("xg", [P, 2, TPC * F])
        mv = sb("mv", [P, 2, TPC, NF + HI])
        oh = sb("oh", [P, 2, TPC * P])
        msg = sb("msg", [P, TPC, F])

        arena = sb("arena", [P, 23 * 2 * CH + 2])

        def area(k, n=2 * CH):
            return arena[:, k * 2 * CH:k * 2 * CH + n]

        dst_i = area(0, T).bitcast(i32)
        nxt_i = area(1, T).bitcast(i32)
        row_i = area(2, T).bitcast(i32)
        prv_i = area(3, T).bitcast(i32)
        dhi_i = area(4, T).bitcast(i32)
        dhi = area(5, T)
        start = area(6, T)
        kb3_f = area(7, W)
        kb3_r = area(8, W)
        kb3_h = area(9, W // 2).bitcast(bf16)
        kb3_m = area(10, W // 2).bitcast(bf16)
        e6 = [arena[0:D6 + 1, (15 + k) * 1024:(15 + k) * 1024 + CH] for k in range(2)]
        h1 = [area(11 + k, CH) for k in range(2)]
        h2 = [area(13 + k, CH) for k in range(2)]
        e16 = [arena[0:D16 + 1, k * CH:(k + 1) * CH] for k in range(2)]
        neg = [area(1, CH), arena[:, 3 * CH:4 * CH]]
        xr = [area(2), area(3)]
        e2, u = area(4), area(5)
        e1 = [area(6), area(7)]
        dd = [area(8), area(9)]
        rel = area(10)
        aa, bb = [area(11), area(12)], [area(13), area(14)]
        be, rr = area(15), area(16)
        ss, qq = area(17), area(18)
        res = area(19)
        xe = [arena[:, (21 + k) * 2 * CH + 2:(22 + k) * 2 * CH + 2] for k in range(2)]
        mm = arena[:, 20 * 2 * CH:20 * 2 * CH + 2 * (CH + 1)].rearrange("p (h n) -> p h n", h=2)
        carry = sb("carry", [P, 4])
        hb = [area(k, CH) for k in range(4)]
        prod = area(4)
        h3 = [arena[0:EH + 1, (5 + k) * 2 * CH:(5 + k) * 2 * CH + CH] for k in range(2)]
        m6 = [arena[0:D6 + 1, (7 + k) * 2 * CH:(7 + k) * 2 * CH + CH] for k in range(2)]

        psum = ctx.enter_context(nc.psum_tensor("psum", [P, 8 * CH], f32))

        def bank(k, n=CH):
            return psum[:, k * CH:k * CH + n]

        ps_x, ps_wa, ps_wm = bank(0, 2 * CH), bank(2, 2 * CH), bank(4, 2 * CH)
        ps_msg = bank(6, TPC * F)
        ps_w = [bank(0, 2 * CH), bank(2, 2 * CH)]
        ps_t, ps_o = bank(4), bank(5)
        ps_h3 = [bank(4), bank(5)]
        ps_agg = bank(7)

        loaded = sem("loaded")
        edges_loaded = sem("edges_loaded")
        consts_made = sem("consts_made")
        start_made = sem("start_made")
        start_stored = sem("start_stored")
        setup_chain = sem("setup_chain")
        setup_done = sem("setup_done")
        n_e6 = sems("n_e6_loaded", 2)
        n_e6_free = sem("n_e6_free")
        n_h1ps, n_h1, n_h2ps, n_h2 = sem("n_h1ps"), sem("n_h1"), sem("n_h2ps"), sem("n_h2")
        n_h1ps_free, n_h1_free = sem("n_h1ps_free"), sem("n_h1_free")
        n_stored = sems("n_h2_stored", 2)
        idx_ready = sem("idx_ready")
        xg_loaded = sems("xg_loaded", 2)
        xg_free = sem("xg_free")
        mv_ready = sem("mv_ready")
        mv_free = sem("mv_free")
        agg_ready = sem("agg_ready")
        a_e16 = sems("a_e16_loaded", 2)
        a_neg = sems("a_neg_loaded", 2)
        a_e16_free, a_neg_free = sem("a_e16_free"), sem("a_neg_free")
        a_w, a_w_free = sem("a_w_ready"), sem("a_w_free")
        a_xe, a_xe_free = sem("a_xe_ready"), sem("a_xe_free")
        a_x = sem("a_x_ready")
        a_xr, a_xr_free = sem("a_xr_ready"), sem("a_xr_free")
        a_d, a_d_free = sem("a_d_ready"), sem("a_d_free")
        a_ab, a_ab_free = sem("a_ab_ready"), sem("a_ab_free")
        a_act = sem("a_act_chain")
        a_res = sem("a_res_ready")
        a_msg, a_msg_free = sem("a_msg_ready"), sem("a_msg_free")
        a_chain_a, a_chain_b, a_chain_c = sem("a_chain_front"), sem("a_chain_sums"), sem("a_chain_spread")
        hb_loaded = sems("hb_loaded", 2)
        hb_free = sem("hb_free")
        m6_loaded = sems("m6_loaded", 2)
        m6_free = sem("m6_free")
        h3ps_ready, h3ps_free = sem("h3ps_ready"), sem("h3ps_free")
        h3_ready, h3_free = sem("h3_ready"), sem("h3_free")
        bias_rows = sem("bias_rows")
        w_ready = sem("w_ready")
        w_free = sem("w_free")
        m_chain = sem("message_chain")
        z_ready, zt_ready, zt_copied, dense_ready = sem("z_ready"), sem("zt_ready"), sem("zt_copied"), sem("dense_ready")
        col_in, col_out = sem("col_in"), sem("col_out")
        act_in, act_out = sem("act_in"), sem("act_out")
        node_chain = sem("node_chain")
        nodes_ready = sem("nodes_ready")
        table_stored = sem("table_stored")
        out_stored = sem("out_stored")

        N_LOADS = 14
        block = ctx.enter_context(nc.Block())

        @block.sync
        def _(sp):
            for dst_ap, src_ap in ((dst_i, dst_t), (nxt_i, dst_next_t), (row_i, dst_row),
                                   (prv_i, dst_prev_row), (src_sb[:, :], src_t)):
                sp.dma_start(dst_ap, src_ap).then_inc(edges_loaded, 16)
            sp.dma_start(kw1_sb[:, :], kw1).then_inc(loaded, 16)
            sp.dma_start(kw2_sb[:, :], kw2).then_inc(loaded, 16)
            sp.dma_start(kb2_sb[:, :], kb2).then_inc(loaded, 16)
            sp.dma_start(con[:, :], consts).then_inc(loaded, 16)
            sp.dma_start(kw3_sb[:, :], kw3).then_inc(loaded, 16)
            sp.dma_start(kb3_f, kb3.partition_broadcast(P)).then_inc(loaded, 16)
            sp.dma_start(wa_sb[:, :], w_attn).then_inc(loaded, 16)
            sp.dma_start(wm_sb[:, :], w_msg).then_inc(loaded, 16)
            sp.dma_start(l3w1_sb[:, :], l3w1).then_inc(loaded, 16)
            sp.dma_start(l3w2_sb[:, :], l3w2).then_inc(loaded, 16)
            sp.dma_start(nw[:, :, :], node_w).then_inc(loaded, 16)
            sp.dma_start(nb[:, :, :], node_b).then_inc(loaded, 16)
            sp.dma_start(eps_sb[:, :], eps).then_inc(loaded, 16)
            sp.wait_ge(consts_made, 1)
            sp.dma_start(xn[:, 0:(HI - 1) * F].rearrange("p (h f) -> p h f", f=F),
                         x[0:(HI - 1) * P, :].rearrange("(h p) f -> p h f", p=P)).then_inc(loaded, 16)
            sp.dma_start(xn[0:N - (HI - 1) * P, (HI - 1) * F:NF], x[(HI - 1) * P:N, :]).then_inc(loaded, 16)

            sp.wait_ge(start_made, 1)
            sp.dma_start(start_d.rearrange("(p t) -> p t", p=P), start).then_inc(start_stored, 16)

            def load_e6(c, b, r):
                sp.wait_ge(n_e6_free, c + 1)
                sp.dma_start(e6[b], ef6[:, bass.ds(c * CH, CH)]).then_inc(n_e6[b], 16)

            def store_h2(c, b, r):
                sp.wait_ge(n_h2, c + 1)
                sp.dma_start(h2_d[bass.ds(c, 1), :, :].rearrange("o p n -> (o p) n"), h2[b]).then_inc(n_stored[b], 16)

            pipeline(sp, [(load_e6, 0), (store_h2, 2)])

            sp.wait_ge(setup_done, 1)
            sp.wait_ge(start_stored, 16)
            for b in range(2):
                sp.wait_ge(n_stored[b], 16 * (C // 2))

            def load_l0(c, b, r):
                sp.wait_ge(a_e16_free, c + 1)
                sp.dma_start(e16[b], ef16[:, bass.ds(c * CH, CH)]).then_inc(a_e16[b], 16)
                sp.wait_ge(a_neg_free, c + 1)
                sp.dma_start(neg[b], start_d[bass.ds(c * CH, CH)].partition_broadcast(P)).then_inc(a_neg[b], 16)

            pipeline(sp, [(load_l0, 0)])

            for p in range(1, PHASES):
                sp.wait_ge(nodes_ready, p)
                sp.dma_start(tables[p].rearrange("(h p) f -> p h f", p=P),
                             nodes[:, 0:NF].rearrange("p (h f) -> p h f", f=F)).then_inc(table_stored, 16)
                if p < L2:
                    def load_hidden(c, b, r, p=p):
                        sp.wait_ge(hb_free, c + (p - 1) * C + 1)
                        sp.dma_start(hb[b], h2_d[bass.ds(c, 1), :, :].rearrange("o p n -> (o p) n"))\
                          .then_inc(hb_loaded[b], 16)

                    pipeline(sp, [(load_hidden, 0)])
                if p == L3:
                    def load_m6(c, b, r):
                        sp.wait_ge(m6_free, c + 1)
                        sp.dma_start(m6[b], ef6[:, bass.ds(c * CH, CH)]).then_inc(m6_loaded[b], 16)

                    pipeline(sp, [(load_m6, 0)])
            sp.wait_ge(nodes_ready, PHASES)
            sp.dma_start(out[0:(HI - 1) * P, :].rearrange("(h p) f -> p h f", p=P),
                         nodes[:, 0:(HI - 1) * F].rearrange("p (h f) -> p h f", f=F)).then_inc(out_stored, 16)
            sp.dma_start(out[(HI - 1) * P:N, :], nodes[0:N - (HI - 1) * P, (HI - 1) * F:NF]).then_inc(out_stored, 16)
            sp.wait_ge(out_stored, 32)

        @block.gpsimd
        def _(pool):
            pool.wait_ge(edges_loaded, 16 * 5)
            pool.wait_ge(setup_done, 1)
            for p in range(PHASES):
                if p:
                    pool.wait_ge(table_stored, 16 * p)

                def gather(c, b, r, p=p):
                    if p:
                        pool.wait_ge(xg_free, c + (p - 1) * C + 1)
                    elif not (isinstance(c, int) and c < 2):
                        pool.wait_ge(a_xe, c - 1)
                    pool.nop(nofuse=True)
                    g.tensor_copy(idx[:, b, :], src_sb[:, bass.ds(c * TPC, TPC)]).then_inc(idx_ready, 1)
                    pool.wait_ge(idx_ready, c + p * C + 1)
                    pool.nop(nofuse=True)
                    for k in range(TPC):
                        pool.indirect_dma_start(
                            xg[:, b, k * F:(k + 1) * F], None, tables[p],
                            bass.IndirectOffsetOnAxis(ap=idx[:, b, k:k + 1], axis=0)).then_inc(xg_loaded[b], 16)

                def expand(c, b, r):
                    pool.wait_ge(xg_loaded[b], (r + 1) * (16 * TPC))
                    pool.wait_ge(a_xe_free, c + 1)
                    pool.nop(nofuse=True)
                    g.tensor_copy(xe[b].rearrange("p (k i o) -> p k i o", i=F, o=F),
                                  xg[:, b, :].rearrange("p (k i) -> p k i", i=F).unsqueeze(3).broadcast_to([P, TPC, F, F]))\
                     .then_inc(a_xe, 1)

                pipeline(pool, [(gather, 0)] if p else [(gather, 0), (expand, 1)])

        @block.scalar
        def _(act):
            act.sem_inc(n_h1ps_free, 2)
            act.sem_inc(a_d_free, 2)
            act.sem_inc(h3ps_free, 2)
            act.wait_ge(loaded, 16 * (N_LOADS + 1))

            def gelu1(c, b, r):
                act.wait_ge(n_h1ps, c + 1)
                act.wait_ge(n_h1_free, c + 1)
                s.activation(h1[b], bank(b), ACT.Gelu_apprx_tanh).then_inc(n_h1, 1)

            def gelu2(c, b, r):
                act.wait_ge(n_h2ps, c + 1)
                if isinstance(c, int) and c < 2:
                    pass
                else:
                    act.wait_ge(n_stored[b], r * 16)
                s.activation(h2[b], bank(2 + b), ACT.Gelu_apprx_tanh, bias=kb2_sb[:, 0:1]).then_inc(n_h2, 1)

            pipeline(act, [(gelu1, 0), (gelu2, 1)])

            for b in range(2):
                act.wait_ge(n_stored[b], 16 * (C // 2))

            def copy_x(c, b, r):
                act.wait_ge(a_x, c + 1)
                act.wait_ge(a_xr_free, c + 1)
                s.copy(xr[b], ps_x).then_inc(a_xr, 1)

            def exps(c, b, r):
                act.wait_ge(a_d, c + 1)
                act.wait_ge(a_ab_free, c + 1)
                if not (isinstance(c, int) and c < 1):
                    act.wait_ge(a_ab, c)
                s.activation(rel, dd[b], ACT.Relu).then_inc(a_act, 1)
                act.wait_ge(a_act, c * 3 + 1)
                s.activation(bb[b], rel, ACT.Exp, scale=-1.0).then_inc(a_act, 1)
                act.wait_ge(a_act, c * 3 + 2)
                s.activation(rel, dd[b], ACT.Relu, scale=-1.0).then_inc(a_act, 1)
                act.wait_ge(a_act, c * 3 + 3)
                s.activation(aa[b], rel, ACT.Exp, scale=-1.0).then_inc(a_ab, 1)

            pipeline(act, [(copy_x, 0), (exps, 1)])

            n_copy = n_fn = 0

            def copy_zt():
                nonlocal n_copy
                n_copy += 1
                act.wait_ge(zt_ready, n_copy)
                s.copy(zt_sb[:, :], ps_t).then_inc(zt_copied, 1)

            def fn(dst_ap, src_ap, func):
                nonlocal n_fn
                n_fn += 1
                act.wait_ge(act_in, n_fn)
                s.activation(dst_ap, src_ap, func).then_inc(act_out, 1)

            fn(st[:, 3, :], st[:, 2, :], ACT.Sqrt)
            for i in range(DEPTH):
                copy_zt()
                fn(nodes[:, 0:NF], t1[:, 0:NF], ACT.Gelu_apprx_tanh)
            fn(st[:, 3, :], st[:, 2, :], ACT.Sqrt)
            for i in range(4):
                copy_zt()
            fn(t2[:, 0:NF], t1[:, 0:NF], ACT.Exp)
            fn(st[:, 3, :], st[:, 2, :], ACT.Ln)
            fn(st[:, 3, :], st[:, 2, :], ACT.Sqrt)

            act.wait_ge(nodes_ready, L3)

            def relu3(c, b, r):
                act.wait_ge(h3ps_ready, c + 1)
                act.wait_ge(h3_free, c + 1)
                s.activation(h3[b][0:EH, :], ps_h3[b][0:EH, :], ACT.Relu).then_inc(h3_ready, 1)

            pipeline(act, [(relu3, 0)])
            fn(fs[:, 3, :], fs[:, 2, :], ACT.Sqrt)
            fn(st[:, 3, :], st[:, 2, :], ACT.Sqrt)

        @block.tensor
        def _(pe):
            pe.sem_inc(n_e6_free, 2)
            pe.sem_inc(n_h1_free, 2)
            pe.sem_inc(a_e16_free, 2)
            pe.sem_inc(a_xe_free, 2)
            pe.sem_inc(m6_free, 2)
            pe.sem_inc(h3_free, 2)
            pe.sem_inc(hb_free, 2)
            pe.sem_inc(mv_free, 2)
            pe.wait_ge(loaded, 16 * (N_LOADS + 1))
            pe.wait_ge(consts_made, 2)

            def first(c, b, r):
                pe.wait_ge(n_e6[b], r * 16 + 16)
                pe.wait_ge(n_h1ps_free, c + 1)
                te.matmul(bank(b), kw1_sb[:, :], e6[b], start=True, stop=True).then_inc(n_h1ps, 1)

            def second(c, b, r):
                pe.wait_ge(n_h1, c + 1)
                pe.sem_inc(n_e6_free, 1)
                pe.sem_inc(n_h1ps_free, 1)
                if not (isinstance(c, int) and c < 2):
                    pe.wait_ge(n_h2, c - 1)
                te.matmul(bank(2 + b), kw2_sb[:, :], h1[b], start=True, stop=True).then_inc(n_h2ps, 1)

            def third(c, b, r):
                pe.wait_ge(n_h2, c + 1)
                pe.sem_inc(n_h1_free, 1)

            pipeline(pe, [(first, 0), (second, 1), (third, 2)])

            def zero_agg():
                te.matmul(ps_agg[:, 0:NF + HI], ones[:, :], zer[:, 0:NF + HI], start=True, stop=False, skip_group_check=True)

            def project(c, b, r):
                pe.wait_ge(a_e16[b], r * 16 + 16)
                pe.wait_ge(a_w_free, c + 1)
                for h in range(2):
                    te.matmul(ps_wa[:, h * CH:(h + 1) * CH], wa_sb[:, h * HALF:(h + 1) * HALF], e16[b], start=True, stop=True)
                for h in range(2):
                    last = te.matmul(ps_wm[:, h * CH:(h + 1) * CH], wm_sb[:, h * HALF:(h + 1) * HALF], e16[b], start=True, stop=True)
                last.then_inc(a_w, 1)
                pe.wait_ge(a_xe, c + 1)
                if not (isinstance(c, int) and c < 1):
                    pe.wait_ge(a_xr, c)
                for h in range(2):
                    for k in range(TPC):
                        last = te.transpose(ps_x[:, h * CH + k * P:h * CH + (k + 1) * P],
                                            xe[b][:, k * W + h * HALF:k * W + (h + 1) * HALF], ident)
                last.then_inc(a_x, 1)
                pe.wait_ge(a_x, c + 1)
                pe.sem_inc(a_e16_free, 1)
                pe.sem_inc(a_xe_free, 1)

            def reduce_i(c, b, r):
                pe.wait_ge(a_res, c + 1)
                pe.wait_ge(a_msg_free, c + 1)
                for k in range(TPC):
                    for h in range(2):
                        last = te.matmul(ps_msg[:, k * F:(k + 1) * F], res[:, h * CH + k * P:h * CH + (k + 1) * P], sel,
                                         start=(h == 0), stop=(h == 1))
                last.then_inc(a_msg, 1)

            def scatter_of(p, cols):
                def scatter(c, b, r):
                    pe.wait_ge(mv_ready, c + p * C + 1)
                    for k in range(TPC):
                        last = te.matmul(ps_agg[:, 0:cols], oh[:, b, k * P:(k + 1) * P], mv[:, b, k, 0:cols],
                                         start=False, stop=False, skip_group_check=True)
                    last.then_inc(mv_free, 1)
                return scatter

            def end_agg(p):
                te.matmul(ps_agg[:, 0:NF + HI], ones[:, :], zer[:, 0:NF + HI], start=False, stop=True,
                          skip_group_check=True).then_inc(agg_ready, 1)

            pe.wait_ge(n_h2, C)
            zero_agg()
            pipeline(pe, [(project, 0), (reduce_i, 2), (scatter_of(L0, NF + HI), 3)], lead=4)
            end_agg(L0)

            n_dense = 0

            def dense(wi):
                nonlocal n_dense
                n_dense += 1
                pe.wait_ge(z_ready, n_dense)
                for q in range(4):
                    last = te.transpose(ps_t[:, q * P:(q + 1) * P], nodes[:, q * P:(q + 1) * P], ident)
                last.then_inc(zt_ready, 1)
                pe.wait_ge(zt_copied, n_dense)
                for q in range(4):
                    last = te.matmul(ps_o[:, q * P:(q + 1) * P], zt_sb[:, q * P:(q + 1) * P], nw[:, wi, :], start=True, stop=True)
                last.then_inc(dense_ready, 1)

            for p in range(1, PHASES):
                pe.wait_ge(nodes_ready, p)
                zero_agg()
                stages = []
                if p < L2:
                    def weights(c, b, r, p=p, wp=p - 1):
                        pe.wait_ge(hb_loaded[b], (r + (p - 1) * (C // 2) + 1) * 16)
                        pe.wait_ge(w_free, c + wp * C + 1)
                        for k in range(TPC):
                            o = ps_w[b][:, k * W:(k + 1) * W]
                            te.matmul(o, hb[b][:, k * P:(k + 1) * P], kw3_sb[:, :], start=True, stop=False)
                            last = te.matmul(o, ones_rows[:, :], kb3_rows[:, :], start=False, stop=True)
                        last.then_inc(w_ready, 1)
                        pe.wait_ge(w_ready, c + wp * C + 1)
                        pe.sem_inc(hb_free, 1)

                    stages = [(weights, 0)]
                if p == L3:
                    def hidden3(c, b, r):
                        pe.wait_ge(m6_loaded[b], r * 16 + 16)
                        pe.wait_ge(h3ps_free, c + 1)
                        te.matmul(ps_h3[b][0:EH, :], l3w1_sb[:, :], m6[b], start=True, stop=True).then_inc(h3ps_ready, 1)

                    def weights3(c, b, r):
                        pe.wait_ge(h3_ready, c + 1)
                        pe.sem_inc(m6_free, 1)
                        pe.sem_inc(h3ps_free, 1)
                        pe.wait_ge(w_free, c + DEPTH * C + 1)
                        for k in range(TPC):
                            last = te.matmul(ps_w[b][:, k * W:(k + 1) * W], h3[b][:, k * P:(k + 1) * P], l3w2_sb[:, :],
                                             start=True, stop=True)
                        last.then_inc(w_ready, 1)
                        pe.wait_ge(w_ready, c + DEPTH * C + 1)
                        pe.sem_inc(h3_free, 1)

                    pe.wait_ge(bias_rows, 1)
                    stages = [(hidden3, 0), (weights3, 1)]
                pipeline(pe, stages + [(scatter_of(p, NF), 2)])
                end_agg(p)
                if p < L2:
                    dense(W_ROOT + p - 1)
                elif p == L2:
                    dense(W_1A)
                    dense(W_1B)
                elif p == L2 + 1:
                    dense(W_2A)
                    dense(W_2B)
                else:
                    for k in range(2):
                        pe.wait_ge(col_in, k + 1)
                        te.matmul(ps_o[:, 0:NF], ones[:, :], t1[:, 0:NF], start=True, stop=True).then_inc(col_out, 1)

        @block.vector
        def _(dve):
            dve.sem_inc(a_neg_free, 2)
            dve.sem_inc(a_w_free, 1)
            dve.sem_inc(a_xr_free, 2)
            dve.sem_inc(a_ab_free, 2)
            dve.sem_inc(a_msg_free, 1)
            dve.sem_inc(xg_free, 2)
            dve.sem_inc(w_free, 2)

            def linker(chain, base):
                n = [0]

                def done(op, wait=True):
                    n[0] += 1
                    op.then_inc(chain, 1)
                    if wait:
                        dve.wait_ge(chain, base + n[0])
                return done

            done = linker(setup_chain, 0)
            v.memset(xn[:, :], 0.0).then_inc(consts_made, 1)
            done(v.memset(nodes[:, :], 0.0), False)
            done(v.memset(zer[:, :], 0.0), False)
            done(v.memset(ones[:, :], 1.0), False)
            done(v.memset(kb3_rows[:, :], 0.0), False)
            done(v.memset(ones_rows[:, :], 0.0), False)
            done(v.memset(carry[:, :], 0.0), False)
            done(v.memset(st[:, :, :], 0.0))
            dve.wait_ge(loaded, 16 * (N_LOADS + 1))
            done(v.tensor_copy(kb3_h, kb3_f))
            done(v.tensor_tensor(kb3_r, kb3_f, kb3_h, ALU.subtract))
            done(v.tensor_copy(kb3_m, kb3_r))
            done(v.tensor_tensor(kb3_r, kb3_r, kb3_m, ALU.subtract))
            for row, part in ((0, kb3_h), (32, kb3_m), (64, kb3_r)):
                done(v.tensor_copy(kb3_rows[row:row + 1, :], part[row:row + 1, :]))
                done(v.memset(ones_rows[row:row + 1, :], 1.0))
            dve.sem_inc(consts_made, 1)
            dve.wait_ge(edges_loaded, 16 * 5)
            done(v.tensor_tensor(start, row_i, prv_i, ALU.not_equal))
            v.tensor_scalar(start, start, NEG, None, ALU.mult).then_inc(start_made, 1)
            done(v.tensor_tensor(is_end[:, :], dst_i, nxt_i, ALU.not_equal))
            done(v.tensor_scalar(dhi_i, dst_i, 7, None, ALU.arith_shift_right))
            done(v.tensor_copy(dhi, dhi_i))
            done(v.tensor_scalar(dhi_i, dst_i, P - 1, None, ALU.bitwise_and))
            done(v.tensor_copy(dlo[:, :], dhi_i))
            done(v.tensor_tensor(ohi[:, :, :], iota[:, 0:HI].unsqueeze(1).broadcast_to([P, T, HI]),
                                 dhi.unsqueeze(2).broadcast_to([P, T, HI]), ALU.is_equal))
            dve.wait_ge(start_stored, 16)
            for b in range(2):
                dve.wait_ge(n_stored[b], 16 * (C // 2))
            done(v.memset(mm[:, :, 0:1], 0.0))
            dve.sem_inc(setup_done, 1)

            def spread(c, b, p, done, m_ap):
                dve.wait_ge(mv_free, c + p * C + 1)
                hot = ohi[:, bass.ds(c * TPC, TPC), :]
                done(v.tensor_tensor(mv[:, b, :, 0:NF].rearrange("p k (h f) -> p k h f", f=F),
                                     m_ap.unsqueeze(2).broadcast_to([P, TPC, HI, F]),
                                     hot.unsqueeze(3).broadcast_to([P, TPC, HI, F]), ALU.mult), False)
                if p == L0:
                    done(v.tensor_copy(mv[:, b, :, NF:NF + HI], hot), False)
                done(v.tensor_tensor(oh[:, b, :].rearrange("p (k n) -> p k n", k=TPC),
                                     iota.unsqueeze(1).broadcast_to([P, TPC, P]),
                                     dlo[:, bass.ds(c * TPC, TPC)].unsqueeze(2).broadcast_to([P, TPC, P]), ALU.is_equal))
                dve.sem_inc(mv_ready, 1)

            KA, KB, KC = 7, 6, 4

            def front(c, b, r):
                done = linker(a_chain_a, c * KA)
                dve.wait_ge(a_w, c + 1)
                dve.wait_ge(a_xr, c + 1)
                done(v.tensor_tensor(e2, ps_wa, xr[b], ALU.mult), False)
                done(v.tensor_tensor(e1[b], ps_wm, xr[b], ALU.mult))
                dve.sem_inc(a_w_free, 1)
                dve.sem_inc(a_xr_free, 1)
                dve.wait_ge(a_neg[b], r * 16 + 16)
                for h in range(2):
                    done(v.tensor_tensor_scan(mm[:, h, 1:CH + 1], neg[b], e2[:, h * CH:(h + 1) * CH],
                                              mm[:, h, 0:1], ALU.add, ALU.max), h == 1)
                done(v.tensor_tensor(u.rearrange("p (h n) -> p h n", h=2), mm[:, :, 0:CH],
                                     neg[b].unsqueeze(1).broadcast_to([P, 2, CH]), ALU.add))
                dve.sem_inc(a_neg_free, 1)
                dve.wait_ge(a_d_free, c + 1)
                done(v.tensor_tensor(dd[b], u, e2, ALU.subtract), False)
                done(v.tensor_copy(mm[:, :, 0:1], mm[:, :, CH:CH + 1]))
                dve.sem_inc(a_d, 1)

            def sums(c, b, r):
                done = linker(a_chain_b, c * KB)
                dve.wait_ge(a_ab, c + 1)
                dve.sem_inc(a_d_free, 1)
                if not (isinstance(c, int) and c < 1):
                    dve.wait_ge(a_msg, c)
                for h in range(2):
                    done(v.tensor_tensor_scan(ss[:, h * CH:(h + 1) * CH], aa[b][:, h * CH:(h + 1) * CH], bb[b][:, h * CH:(h + 1) * CH],
                                              carry[:, h:h + 1], ALU.mult, ALU.add), False)
                done(v.tensor_tensor(be, bb[b], e1[b], ALU.mult))
                for h in range(2):
                    done(v.tensor_tensor_scan(qq[:, h * CH:(h + 1) * CH], aa[b][:, h * CH:(h + 1) * CH], be[:, h * CH:(h + 1) * CH],
                                              carry[:, 2 + h:3 + h], ALU.mult, ALU.add), False)
                done(v.reciprocal(rr, ss))
                dve.sem_inc(a_ab_free, 1)
                for k, src_ap in ((0, ss), (2, qq)):
                    v.tensor_copy(carry[:, k:k + 2].unsqueeze(2), src_ap.rearrange("p (h n) -> p h n", h=2)[:, :, CH - 1:CH])
                v.tensor_tensor(res, qq, rr, ALU.mult).then_inc(a_res, 1)
                dve.wait_ge(a_res, c + 1)

            def emit(c, b, r):
                done = linker(a_chain_c, c * KC)
                dve.wait_ge(a_msg, c + 1)
                done(v.tensor_tensor(msg[:, :, :], ps_msg.rearrange("p (k f) -> p k f", f=F),
                                     is_end[:, bass.ds(c * TPC, TPC)].unsqueeze(2).broadcast_to([P, TPC, F]), ALU.mult))
                dve.sem_inc(a_msg_free, 1)
                spread(c, b, L0, done, msg[:, :, :])

            pipeline(dve, [(front, 0), (emit, 3), (sums, 1)], lead=4)

            done = linker(node_chain, 0)
            n_z = n_fn = n_col = 0

            def blocks(ap):
                return ap.rearrange("p (h f) -> p h f", f=F)

            def over_f(ap):
                return ap.unsqueeze(2).broadcast_to([P, HI, F])

            def over_h(ap):
                return ap.unsqueeze(1).broadcast_to([P, HI, F])

            N1, N2, ND = blocks(t1[:, 0:NF]), blocks(t2[:, 0:NF]), blocks(nodes[:, 0:NF])
            XN, AGG, DENSE = blocks(xn[:, 0:NF]), blocks(ps_agg[:, 0:NF]), blocks(ps_o[:, 0:NF])

            def function():
                nonlocal n_fn
                n_fn += 1
                dve.sem_inc(act_in, 1)
                dve.wait_ge(act_out, n_fn)

            def dense():
                nonlocal n_z
                n_z += 1
                dve.sem_inc(z_ready, 1)
                dve.wait_ge(dense_ready, n_z)

            def layernorm():
                done(v.tensor_reduce(st[:, 0, :], N1, X, ALU.add))
                done(v.tensor_scalar(st[:, 1, :], st[:, 0, :], 1.0 / F, None, ALU.mult))
                done(v.tensor_tensor(N1, N1, over_f(st[:, 1, :]), ALU.subtract))
                done(v.tensor_tensor(N2, N1, N1, ALU.mult))
                done(v.tensor_reduce(st[:, 0, :], N2, X, ALU.add))
                done(v.tensor_scalar(st[:, 2, :], st[:, 0, :], 1.0 / F, LN_EPS, ALU.mult, ALU.add))
                function()
                done(v.reciprocal(st[:, 4, :], st[:, 3, :]))
                done(v.tensor_tensor(ND, N1, over_f(st[:, 4, :]), ALU.mult))
                done(v.tensor_copy(xn[:, 0:NF], nodes[:, 0:NF]))

            dve.wait_ge(agg_ready, 1)
            deg = ps_agg[:, NF:NF + HI]
            done(v.tensor_scalar(st[:, 0, :], deg, 1.0, None, ALU.max))
            done(v.reciprocal(inv_deg1[:, :], st[:, 0, :]))
            done(v.tensor_scalar(st[:, 1, :], deg, 0.0, None, ALU.is_gt))
            done(v.tensor_tensor(inv_deg[:, :], st[:, 1, :], inv_deg1[:, :], ALU.mult))
            done(v.tensor_tensor(N1, AGG, XN, ALU.add))
            layernorm()
            dve.sem_inc(nodes_ready, 1)

            base = 0
            for p in range(1, PHASES):
                if p == L3:
                    for b in range(2):
                        done(v.memset(arena[EH:EH + 1, (5 + b) * 2 * CH:(5 + b) * 2 * CH + CH], 1.0))
                    dve.sem_inc(bias_rows, 1)
                KM = 4 if p not in (L2, L2 + 1) else 2
                wp = p - 1 if p < L2 else DEPTH

                def message(c, b, r, p=p, KM=KM, wp=wp, base=base):
                    done = linker(m_chain, c * KM + base)
                    dve.wait_ge(xg_loaded[b], (r + p * (C // 2) + 1) * (16 * TPC))
                    rows = xg[:, b, :].rearrange("p (k f) -> p k f", f=F)
                    if p in (L2, L2 + 1):
                        spread(c, b, p, done, rows)
                        dve.sem_inc(xg_free, 1)
                        return
                    dve.wait_ge(w_ready, c + wp * C + 1)
                    done(v.tensor_tensor(prod.rearrange("p (k i o) -> p k i o", i=F, o=F),
                                         ps_w[b].rearrange("p (k i o) -> p k i o", i=F, o=F),
                                         rows.unsqueeze(3).broadcast_to([P, TPC, F, F]), ALU.mult))
                    dve.sem_inc(w_free, 1)
                    dve.sem_inc(xg_free, 1)
                    done(v.tensor_reduce(msg[:, :, :], prod.rearrange("p (k i o) -> p k o i", i=F, o=F), X, ALU.add))
                    spread(c, b, p, done, msg[:, :, :])

                pipeline(dve, [(message, 0)])
                base += KM * C
                dve.wait_ge(agg_ready, p + 1)
                if p < L2:
                    done(v.tensor_tensor(N1, AGG, over_f(inv_deg[:, :]), ALU.mult))
                    dense()
                    done(v.tensor_tensor(N1, N1, DENSE, ALU.add))
                    done(v.tensor_tensor(N1, N1, over_h(nb[:, B_ROOT + p - 1, :]), ALU.add))
                    function()
                    if p == L2 - 1:
                        done(v.tensor_tensor(N1, XN, ND, ALU.add))
                        layernorm()
                elif p < L3:
                    q = p - L2
                    done(v.tensor_scalar(st[:, 0, 0:1], eps_sb[:, q:q + 1], 1.0, None, ALU.add))
                    done(v.tensor_scalar(t1[:, 0:NF], nodes[:, 0:NF], st[:, 0, 0:1], None, ALU.mult))
                    done(v.tensor_tensor(ND, N1, AGG, ALU.add))
                    dense()
                    done(v.tensor_tensor(N1, DENSE, over_h(nb[:, B_1A + 2 * q, :]), ALU.add))
                    done(v.tensor_scalar(nodes[:, 0:NF], t1[:, 0:NF], 0.0, None, ALU.max))
                    dense()
                    done(v.tensor_tensor(N1, DENSE, over_h(nb[:, B_1B + 2 * q, :]), ALU.add))
                    if q == 0:
                        done(v.tensor_scalar(nodes[:, 0:NF], t1[:, 0:NF], 0.0, None, ALU.max))
                    else:
                        done(v.tensor_reduce(st[:, 0, :], N1, X, ALU.max))
                        done(v.tensor_tensor(N1, N1, over_f(st[:, 0, :]), ALU.subtract))
                        function()
                        done(v.tensor_reduce(st[:, 2, :], N2, X, ALU.add))
                        function()
                        done(v.tensor_tensor(N1, N1, over_f(st[:, 3, :]), ALU.subtract))
                        done(v.tensor_tensor(N1, N1, XN, ALU.add))
                        layernorm()
                else:
                    done(v.tensor_tensor(N1, AGG, over_f(inv_deg1[:, :]), ALU.mult))
                    done(v.tensor_tensor(N1, N1, over_h(nb[:, B_BIAS, :]), ALU.add))
                    done(v.tensor_scalar(t1[:, 0:NF], t1[:, 0:NF], 0.0, None, ALU.max))
                    done(v.tensor_tensor(N1, N1, over_f(valid), ALU.mult))
                    for k in range(2):
                        dve.sem_inc(col_in, 1)
                        dve.wait_ge(col_out, k + 1)
                        done(v.tensor_reduce(fs[:, 0, :], ps_o[:, 0:NF].rearrange("p (h f) -> p f h", f=F), X, ALU.add))
                        if k == 0:
                            done(v.tensor_scalar(fs[:, 1, :], fs[:, 0, :], 1.0 / N, None, ALU.mult))
                            done(v.tensor_tensor(ND, N1, over_h(fs[:, 1, :]), ALU.subtract))
                            done(v.tensor_tensor(N2, ND, over_f(valid), ALU.mult))
                            done(v.tensor_tensor(N1, N2, N2, ALU.mult))
                    done(v.tensor_scalar(fs[:, 2, :], fs[:, 0, :], 1.0 / N, BN_EPS, ALU.mult, ALU.add))
                    function()
                    done(v.reciprocal(fs[:, 1, :], fs[:, 3, :]))
                    done(v.tensor_tensor(fs[:, 0, :], fs[:, 1, :], nb[:, B_GAMMA, :], ALU.mult))
                    done(v.tensor_tensor(N1, ND, over_h(fs[:, 0, :]), ALU.mult))
                    done(v.tensor_tensor(N1, N1, over_h(nb[:, B_BETA, :]), ALU.add))
                    done(v.tensor_tensor(N1, N1, XN, ALU.add))
                    layernorm()
                dve.sem_inc(nodes_ready, 1)


_OUT = ((N, F), 'float32')


def kernel(**inputs):
    import numpy as np
    import concourse.bacc as bacc
    from concourse.bass_utils import run_bass_kernel_spmd as run

    a = {k: np.asarray(val) for k, val in inputs.items()}

    def tiles(row):
        return np.ascontiguousarray(row.reshape(T, P).T)

    def with_bias(w, b):
        return np.concatenate([w, b[None, :]], axis=0)

    def padded(attr):
        d = attr.shape[1]
        o = np.zeros((d + 1, EP), np.float32)
        o[:d, :E] = attr.T
        o[d] = 1.0
        return o

    src = np.zeros(EP, np.int32)
    src[:E] = a['src']
    dst = np.full(EP, NPAD, np.int32)
    dst[:E] = a['dst']
    nxt = np.full(EP, -1, np.int32)
    nxt[:-1] = dst[1:]
    prv = np.full(EP, -1, np.int32)
    prv[1:] = dst[:-1]

    mats = list(a['L1_gnn_root_W']) + [a[f'L2_gnn_{k}'] for k in ('w1a', 'w1b', 'w2a', 'w2b')]
    node_w = np.zeros((P, NWM, P), np.float32)
    for n, m in enumerate(mats):
        for q in range(P // F):
            node_w[q * F:(q + 1) * F, n, q * F:(q + 1) * F] = m
    rows = list(a['L1_gnn_root_b']) + [a[f'L2_gnn_{k}'] for k in ('b1a', 'b1b', 'b2a', 'b2b')] + \
        [a[f'L3_gnn_{k}'] for k in ('bias', 'gamma', 'beta')]
    node_b = np.ascontiguousarray(np.broadcast_to(np.stack(rows), (P, NBR, F)))
    eps = np.ascontiguousarray(np.broadcast_to(np.stack([a['L2_gnn_eps1'], a['L2_gnn_eps2']]), (P, 2)))

    consts = np.zeros((P, NK), np.float32)
    consts[:, K_ID:K_ID + P] = np.eye(P)
    consts[:, K_IOTA:K_IOTA + P] = np.arange(P)
    consts[np.arange(P), K_SEL + np.arange(P) % F] = 1.0
    consts[:, K_VALID:K_VALID + HI] = (np.arange(HI)[None, :] * P + np.arange(P)[:, None]) < N

    data = {
        'x': a['x'], 'src_t': tiles(src), 'dst_t': tiles(dst), 'dst_next_t': tiles(nxt),
        'dst_row': dst.reshape(P, T), 'dst_prev_row': prv.reshape(P, T),
        'ef16': padded(a['edge_attr_16']), 'ef6': padded(a['edge_attr_6']),
        'w_attn': with_bias(a['L0_gnn_W_attn'], a['L0_gnn_b_attn']),
        'w_msg': with_bias(a['L0_gnn_W_msg'], a['L0_gnn_b_msg']),
        'kw1': with_bias(a['L1_gnn_kW1'], a['L1_gnn_kb1']),
        'kw2': a['L1_gnn_kW2'], 'kb2': a['L1_gnn_kb2'].reshape(KD, 1),
        'kw3': a['L1_gnn_kW3'], 'kb3': a['L1_gnn_kb3'],
        'l3w1': with_bias(a['L3_gnn_W1'], a['L3_gnn_b1']),
        'l3w2': with_bias(a['L3_gnn_W2'], a['L3_gnn_b2']),
        'node_w': node_w, 'node_b': node_b, 'eps': eps, 'consts': consts,
    }
    nc = bacc.Bacc("TRN2", target_bir_lowering=False, num_devices=1)
    arrays, args = {}, []
    for name, val in data.items():
        val = np.ascontiguousarray(val)
        arrays[f"in_{name}"] = val
        args.append(nc.dram_tensor(f"in_{name}", val.shape, mybir.dt.from_np(val.dtype), kind="ExternalInput").ap())
    out = nc.dram_tensor("out_nodes", _OUT[0], mybir.dt.from_np(np.dtype(_OUT[1])), kind="ExternalOutput").ap()
    gnn_resnorm(nc, *args, out)
    r = run(nc, [arrays], core_ids=[0])
    return r.results[0]["out_nodes"]
```

```python
import concourse.bass as bass
from concourse import mybir
from contextlib import ExitStack

N = 3125
E = 103125
F = 16
P = 128
HI = -(-N // P)
NF = HI * F
NPAD = HI * P
CH = 512
TPC = CH // P
C = 4 * (-(-E // (4 * CH)))
T = C * TPC
EP = C * CH
W = F * F
HALF = W // 2
KD = 128
EH = 64
D16, D6 = 16, 6
DEPTH = 4
LN_EPS = 1e-5
BN_EPS = 1e-5
NEG = -3.0e38
FAR = 1 << 20
PHASES = 1 + DEPTH + 2 + 1
L0, L1, L2, L3 = 0, 1, 1 + DEPTH, 3 + DEPTH

W_ROOT, W_1A, W_1B, W_2A, W_2B, NWM = 0, 4, 5, 6, 7, 8
B_ROOT, B_1A, B_1B, B_2A, B_2B, B_BIAS, B_GAMMA, B_BETA, NBR = 0, 4, 5, 6, 7, 8, 9, 10, 11
K_ID, K_IOTA, K_SEL, K_VALID, NK = 0, P, 2 * P, 2 * P + F, 2 * P + F + HI


def pipeline(eng, stages, lead=4):
    for c in range(lead):
        for stage, lag in stages:
            if c >= lag:
                stage(c - lag, (c - lag) % 4, (c - lag) // 4)
    with eng.Fori(0, (C - lead) // 4) as i:
        for j in range(4):
            for stage, lag in stages:
                at = lead + j - lag
                stage(i * 4 + at, at % 4, i + at // 4)
    for c in range(C, C + max(lag for _, lag in stages)):
        for stage, lag in stages:
            if c - lag < C:
                stage(c - lag, (c - lag) % 4, (c - lag) // 4)


def turn(b, r):
    return r * 2 + b // 2


def started(c, n):
    return not isinstance(c, int) or c >= n


def gnn_resnorm(nc, x, src_t, dst_t, dst_next_t, dst_row, dst_prev_row, ef16, ef6, w_attn, w_msg,
                kw1, kw2, kb2, kw3, kb3, l3w1, l3w2, node_w, node_b, eps, consts, out):
    f32, bf16, i32 = mybir.dt.float32, mybir.dt.bfloat16, mybir.dt.int32
    ALU, ACT, X = mybir.AluOpType, mybir.ActivationFunctionType, mybir.AxisListType.X
    v, s, g, te = nc.vector, nc.scalar, nc.gpsimd, nc.tensor

    tables = [x] + [nc.dram_tensor(f"node_table_{p}", (NPAD, F), f32, kind="Internal").ap()
                    for p in range(1, PHASES)]
    start_d = nc.dram_tensor("start_mask", (EP,), f32, kind="Internal").ap()
    sums_d = nc.dram_tensor("softmax_sums", (NPAD, 2 * W), f32, kind="Internal").ap()
    h2_d = nc.dram_tensor("edge_hidden", (C, P, CH), f32, kind="Internal").ap()

    ctx = ExitStack()
    with ctx:
        def sb(name, shape, dt=f32):
            return ctx.enter_context(nc.sbuf_tensor(name, shape, dt))

        def sem(name):
            return ctx.enter_context(nc.semaphore(name))

        def sems(name, n):
            return [sem(f"{name}_{k}") for k in range(n)]

        src_sb = sb("src_sb", [P, T], i32)
        dlo = sb("dlo", [P, T])
        dhi = sb("dhi", [P, T])
        end_row = sb("end_row", [P, T], i32)
        con = sb("con", [P, NK])
        ident, iota = con[:, K_ID:K_ID + P], con[:, K_IOTA:K_IOTA + P]
        sel, valid = con[:, K_SEL:K_SEL + F], con[:, K_VALID:K_VALID + HI]
        nw = sb("nw", [P, NWM, P])
        nb = sb("nb", [P, NBR, F])
        eps_sb = sb("eps_sb", [P, 2])
        zer = sb("zer", [P, CH])
        ones = sb("ones", [P, P])
        wa_sb = sb("wa_sb", [D16 + 1, W])
        wm_sb = sb("wm_sb", [D16 + 1, W])
        kw1_sb = sb("kw1_sb", [D6 + 1, KD])
        kw2_sb = sb("kw2_sb", [P, KD])
        kb2_sb = sb("kb2_sb", [P, 1])
        kw3_sb = sb("kw3_sb", [P, W])
        l3w1_sb = sb("l3w1_sb", [D6 + 1, EH])
        l3w2_sb = sb("l3w2_sb", [EH + 1, W])
        kb3_rows = sb("kb3_rows", [P, W], bf16)
        ones_rows = sb("ones_rows", [P, P], bf16)
        xn = sb("xn", [P, CH])
        nodes = sb("nodes", [P, CH])
        zt_sb = sb("zt_sb", [P, CH])
        t1 = sb("t1", [P, CH])
        t2 = sb("t2", [P, CH])
        st = sb("st", [P, 6, HI])
        fs = sb("fs", [P, 4, F])
        inv_deg = sb("inv_deg", [P, HI])
        inv_deg1 = sb("inv_deg1", [P, HI])
        idx = sb("idx", [P, 4, TPC], i32)
        idx_end = sb("idx_end", [P, 2, TPC], i32)
        xg = sb("xg", [P, 4, TPC * F])
        msg = sb("msg", [P, TPC, F])

        arena = sb("arena", [P, 30 * 2 * CH])

        def area(k, n=2 * CH):
            return arena[:, k * 2 * CH:k * 2 * CH + n]

        def halves(k, rows=P):
            return [arena[0:rows, k * 2 * CH + q * CH:k * 2 * CH + (q + 1) * CH] for q in range(2)]

        dst_i, nxt_i, row_i, prv_i, tmp_i = (area(k, T).bitcast(i32) for k in range(5))
        start, end_f = area(5, T), area(6, T)
        kb3_f, kb3_r = area(7, W), area(8, W)
        kb3_h, kb3_m = (area(k, W // 2).bitcast(bf16) for k in (9, 10))
        e16, neg = halves(0, D16 + 1), halves(1)
        xr = [area(2), area(3)]
        e2, u = area(4), area(5)
        e1 = [area(6), area(7)]
        dd = [area(8), area(9)]
        rel = [area(10), area(11)]
        aa, bb = [area(12), area(13)], [area(14), area(15)]
        be = area(16)
        ss, qq = [area(17), area(18)], [area(19), area(20)]
        xe = [area(21), area(22)]
        rows_sq = [[halves(23 + 2 * q + k // 2)[k % 2] for k in range(TPC)] for q in range(2)]
        mm = arena[:, 27 * 2 * CH:27 * 2 * CH + 2 * (CH + 1)].rearrange("p (h n) -> p h n", h=2)
        sq = arena[:, 0:HI * 2 * W].rearrange("p (h c) -> p h c", h=HI)
        ohi = arena[:, 15 * 1024:15 * 1024 + T * HI // 2].bitcast(bf16).rearrange("p (t h) -> p t h", h=HI)
        hb = halves(0)
        prod = area(1)
        m6 = halves(2, D6 + 1)
        h1 = halves(3)
        h3 = halves(4, EH + 1)
        oh = [halves(5)[q].rearrange("p (k n) -> p k n", k=TPC) for q in range(2)]
        mv = [arena[:, (6 + 2 * q) * 1024:(6 + 2 * q) * 1024 + TPC * (NF + HI)].rearrange("p (k n) -> p k n", k=TPC)
              for q in range(2)]

        psum = ctx.enter_context(nc.psum_tensor("psum", [P, 8 * CH], f32))

        def bank(k, n=CH):
            return psum[:, k * CH:k * CH + n]

        ps_x, ps_wa, ps_wm = bank(0, 2 * CH), bank(2, 2 * CH), bank(4, 2 * CH)
        ps_rows = [bank(6), bank(7)]
        ps_w = [bank(0, 2 * CH), bank(2, 2 * CH)]
        ps_h1, ps_h2 = [bank(4), bank(5)], bank(6)
        ps_t, ps_o = bank(4), bank(5)
        ps_agg = bank(7)

        loaded = sem("loaded")
        edges_loaded = sem("edges_loaded")
        consts_made = sem("consts_made")
        start_made = sem("start_made")
        start_stored = sem("start_stored")
        setup_chain = sem("setup_chain")
        setup_done = sem("setup_done")
        idx_ready = sem("idx_ready")
        xg_loaded = sems("xg_loaded", 4)
        mv_ready = sem("mv_ready")
        mv_free = sem("mv_free")
        agg_ready = sem("agg_ready")
        sums_zeroed = sem("sums_zeroed")
        a_e16 = sems("a_e16_loaded", 2)
        a_neg = sems("a_neg_loaded", 2)
        a_xe, a_x, a_xr = sem("a_xe_ready"), sem("a_x_ready"), sem("a_xr_ready")
        a_wa, a_wm = sem("a_wa_ready"), sem("a_wm_ready")
        a_e2, a_e1, a_m, a_u = sem("a_e2_ready"), sem("a_e1_ready"), sem("a_m_ready"), sem("a_u_ready")
        a_carry, a_d = sem("a_carry_ready"), sem("a_d_ready")
        a_rel, a_ab = sem("a_rel_ready"), sem("a_ab_ready")
        a_be, a_q = sem("a_be_ready"), sem("a_q_ready")
        a_t, a_rows = sem("a_transposed"), sem("a_rows_ready")
        a_end = sem("a_end_index_ready")
        a_sent = sems("a_sums_sent", 2)
        sums_loaded = sem("sums_loaded")
        m6_loaded = sems("m6_loaded", 2)
        n_h1ps, n_h1, n_h2ps, n_h2 = sem("n_h1ps"), sem("n_h1"), sem("n_h2ps"), sem("n_h2")
        n_stored = sems("n_h2_stored", 2)
        hb_loaded = sems("hb_loaded", 2)
        h3ps_ready, h3_ready = sem("h3ps_ready"), sem("h3_ready")
        w_ready = sem("w_ready")
        w_free = sem("w_free")
        m_sum = sem("message_ready")
        bias_rows = sem("bias_rows")
        z_ready, zt_ready, zt_copied, dense_ready = sem("z_ready"), sem("zt_ready"), sem("zt_copied"), sem("dense_ready")
        col_in, col_out = sem("col_in"), sem("col_out")
        act_in, act_out = sem("act_in"), sem("act_out")
        node_chain = sem("node_chain")
        nodes_ready = sem("nodes_ready")
        table_stored = sem("table_stored")
        out_stored = sem("out_stored")

        N_LOADS = 14
        block = ctx.enter_context(nc.Block())

        @block.sync
        def _(sp):
            for dst_ap, src_ap in ((dst_i, dst_t), (nxt_i, dst_next_t), (row_i, dst_row),
                                   (prv_i, dst_prev_row), (src_sb[:, :], src_t)):
                sp.dma_start(dst_ap, src_ap).then_inc(edges_loaded, 16)
            sp.dma_start(kw1_sb[:, :], kw1).then_inc(loaded, 16)
            sp.dma_start(kw2_sb[:, :], kw2).then_inc(loaded, 16)
            sp.dma_start(kb2_sb[:, :], kb2).then_inc(loaded, 16)
            sp.dma_start(con[:, :], consts).then_inc(loaded, 16)
            sp.dma_start(kw3_sb[:, :], kw3).then_inc(loaded, 16)
            sp.dma_start(kb3_f, kb3.partition_broadcast(P)).then_inc(loaded, 16)
            sp.dma_start(wa_sb[:, :], w_attn).then_inc(loaded, 16)
            sp.dma_start(wm_sb[:, :], w_msg).then_inc(loaded, 16)
            sp.dma_start(l3w1_sb[:, :], l3w1).then_inc(loaded, 16)
            sp.dma_start(l3w2_sb[:, :], l3w2).then_inc(loaded, 16)
            sp.dma_start(nw[:, :, :], node_w).then_inc(loaded, 16)
            sp.dma_start(nb[:, :, :], node_b).then_inc(loaded, 16)
            sp.dma_start(eps_sb[:, :], eps).then_inc(loaded, 16)
            sp.wait_ge(consts_made, 1)
            sp.dma_start(xn[:, 0:(HI - 1) * F].rearrange("p (h f) -> p h f", f=F),
                         x[0:(HI - 1) * P, :].rearrange("(h p) f -> p h f", p=P)).then_inc(loaded, 16)
            sp.dma_start(xn[0:N - (HI - 1) * P, (HI - 1) * F:NF], x[(HI - 1) * P:N, :]).then_inc(loaded, 16)

            sp.wait_ge(start_made, 1)
            sp.dma_start(start_d.rearrange("(p t) -> p t", p=P), start).then_inc(start_stored, 16)

            sp.wait_ge(setup_chain, 2)
            sp.dma_start(sums_d.rearrange("(h p) c -> p h c", p=P),
                         zer[:, :].unsqueeze(1).broadcast_to([P, HI, CH])).then_inc(sums_zeroed, 16)

            sp.wait_ge(setup_done, 1)

            def load_l0(c, b, r):
                q = b % 2
                if started(c, 2):
                    sp.wait_ge(a_e1, c - 1)
                sp.dma_start(e16[q], ef16[:, bass.ds(c * CH, CH)]).then_inc(a_e16[q], 16)
                if started(c, 2):
                    sp.wait_ge(a_u, c - 1)
                sp.dma_start(neg[q], start_d[bass.ds(c * CH, CH)].partition_broadcast(P)).then_inc(a_neg[q], 16)

            pipeline(sp, [(load_l0, 0)])
            for q in range(2):
                sp.wait_ge(a_sent[q], 16 * TPC * (C // 2))
            sp.dma_start(sq, sums_d.rearrange("(h p) c -> p h c", p=P)).then_inc(sums_loaded, 16)

            for p in range(1, PHASES):
                sp.wait_ge(nodes_ready, p)
                sp.dma_start(tables[p].rearrange("(h p) f -> p h f", p=P),
                             nodes[:, 0:NF].rearrange("p (h f) -> p h f", f=F)).then_inc(table_stored, 16)

                def load_m6(c, b, r, p=p):
                    q = b % 2
                    if started(c, 2):
                        sp.wait_ge(n_h1 if p == 1 else h3_ready, c - 1)
                    sp.dma_start(m6[q], ef6[:, bass.ds(c * CH, CH)]).then_inc(m6_loaded[q], 16)

                def store_h2(c, b, r):
                    sp.wait_ge(n_h2, c + 1)
                    sp.dma_start(h2_d[bass.ds(c, 1), :, :].rearrange("o p n -> (o p) n"), hb[b % 2]).then_inc(n_stored[b % 2], 16)

                def load_hidden(c, b, r, p=p):
                    sp.wait_ge(w_free, c + (p - 1) * C + 1)
                    sp.dma_start(hb[b % 2], h2_d[bass.ds(c, 1), :, :].rearrange("o p n -> (o p) n"))\
                      .then_inc(hb_loaded[b % 2], 16)

                if p == 1:
                    pipeline(sp, [(load_m6, 0), (store_h2, 3)])
                    for q in range(2):
                        sp.wait_ge(n_stored[q], 16 * (C // 2))
                elif p < L2:
                    pipeline(sp, [(load_hidden, 0)])
                elif p == L3:
                    pipeline(sp, [(load_m6, 0)])
            sp.wait_ge(nodes_ready, PHASES)
            sp.dma_start(out[0:(HI - 1) * P, :].rearrange("(h p) f -> p h f", p=P),
                         nodes[:, 0:(HI - 1) * F].rearrange("p (h f) -> p h f", f=F)).then_inc(out_stored, 16)
            sp.dma_start(out[(HI - 1) * P:N, :], nodes[0:N - (HI - 1) * P, (HI - 1) * F:NF]).then_inc(out_stored, 16)
            sp.wait_ge(out_stored, 32)

        @block.gpsimd
        def _(pool):
            pool.wait_ge(edges_loaded, 16 * 5)
            pool.wait_ge(setup_done, 1)
            for p in range(PHASES):
                if p:
                    pool.wait_ge(table_stored, 16 * p)

                def gather(c, b, r, p=p):
                    if p == L0 and started(c, 4):
                        pool.wait_ge(a_xe, c - 3)
                    elif p in (L2, L2 + 1) and started(c, 4):
                        pool.wait_ge(mv_ready, c + (p - 1) * C - 3)
                    elif started(c, 4):
                        pool.wait_ge(w_free, c + (p - 1 if p < L2 else DEPTH) * C - 1)
                    pool.nop(nofuse=True)
                    g.tensor_copy(idx[:, b, :], src_sb[:, bass.ds(c * TPC, TPC)]).then_inc(idx_ready, 1)
                    pool.wait_ge(idx_ready, c + p * C + 1)
                    pool.nop(nofuse=True)
                    for k in range(TPC):
                        pool.indirect_dma_start(
                            xg[:, b, k * F:(k + 1) * F], None, tables[p],
                            bass.IndirectOffsetOnAxis(ap=idx[:, b, k:k + 1], axis=0)).then_inc(xg_loaded[b], 16)

                def send_sums(c, b, r):
                    q = b % 2
                    if started(c, 2):
                        pool.wait_ge(a_sent[q], turn(b, r) * (16 * TPC))
                    pool.nop(nofuse=True)
                    g.tensor_copy(idx_end[:, q, :], end_row[:, bass.ds(c * TPC, TPC)]).then_inc(a_end, 1)
                    pool.wait_ge(a_end, c + 1)
                    pool.wait_ge(a_rows, c * TPC + TPC)
                    pool.nop(nofuse=True)
                    for k in range(TPC):
                        pool.indirect_dma_start(
                            sums_d, bass.IndirectOffsetOnAxis(ap=idx_end[:, q, k:k + 1], axis=0), rows_sq[q][k], None,
                            bounds_check=NPAD - 1, oob_is_err=False).then_inc(a_sent[q], 16)

                if p == L0:
                    pool.wait_ge(sums_zeroed, 16)
                    pipeline(pool, [(gather, 0), (send_sums, 5)], lead=8)
                else:
                    pipeline(pool, [(gather, 0)])

        @block.scalar
        def _(act):
            act.wait_ge(loaded, 16 * (N_LOADS + 1))

            def expand(c, b, r):
                act.wait_ge(xg_loaded[b], (r + 1) * (16 * TPC))
                if started(c, 2):
                    act.wait_ge(a_x, c - 1)
                s.copy(xe[b % 2].rearrange("p (k i o) -> p k i o", i=F, o=F),
                       xg[:, b, :].rearrange("p (k i) -> p k i", i=F).unsqueeze(3).broadcast_to([P, TPC, F, F]))\
                 .then_inc(a_xe, 1)

            def copy_x(c, b, r):
                act.wait_ge(a_x, c + 1)
                if started(c, 2):
                    act.wait_ge(a_e1, c - 1)
                s.copy(xr[b % 2], ps_x).then_inc(a_xr, 1)

            def exps(c, b, r):
                q = b % 2
                act.wait_ge(a_d, c + 1)
                if started(c, 1):
                    act.wait_ge(a_ab, c)
                s.activation(rel[0], dd[q], ACT.Relu).then_inc(a_rel, 1)
                s.activation(rel[1], dd[q], ACT.Relu, scale=-1.0).then_inc(a_rel, 1)
                if started(c, 2):
                    act.wait_ge(a_q, c - 1)
                act.wait_ge(a_rel, c * 2 + 1)
                s.activation(bb[q], rel[0], ACT.Exp, scale=-1.0)
                act.wait_ge(a_rel, c * 2 + 2)
                s.activation(aa[q], rel[1], ACT.Exp, scale=-1.0).then_inc(a_ab, 1)

            def copy_rows(c, b, r):
                q = b % 2
                if started(c, 2):
                    act.wait_ge(a_sent[q], turn(b, r) * (16 * TPC))
                for k in range(TPC):
                    act.wait_ge(a_t, c * TPC + k + 1)
                    s.copy(rows_sq[q][k], ps_rows[k % 2]).then_inc(a_rows, 1)

            pipeline(act, [(expand, 0), (copy_x, 1), (exps, 2), (copy_rows, 3)], lead=8)

            n_copy = n_fn = 0

            def copy_zt():
                nonlocal n_copy
                n_copy += 1
                act.wait_ge(zt_ready, n_copy)
                s.copy(zt_sb[:, :], ps_t).then_inc(zt_copied, 1)

            def fn(dst_ap, src_ap, func):
                nonlocal n_fn
                n_fn += 1
                act.wait_ge(act_in, n_fn)
                s.activation(dst_ap, src_ap, func).then_inc(act_out, 1)

            fn(st[:, 3, :], st[:, 2, :], ACT.Sqrt)

            def gelu1(c, b, r):
                act.wait_ge(n_h1ps, c + 1)
                if started(c, 2):
                    act.wait_ge(n_h2ps, c - 1)
                s.activation(h1[b % 2], ps_h1[b % 2], ACT.Gelu_apprx_tanh).then_inc(n_h1, 1)

            def gelu2(c, b, r):
                act.wait_ge(n_h2ps, c + 1)
                if started(c, 2):
                    act.wait_ge(n_stored[b % 2], turn(b, r) * 16)
                    act.wait_ge(w_free, c + 1)
                s.activation(hb[b % 2], ps_h2, ACT.Gelu_apprx_tanh, bias=kb2_sb[:, 0:1]).then_inc(n_h2, 1)

            act.wait_ge(nodes_ready, 1)
            pipeline(act, [(gelu1, 0), (gelu2, 1)])
            for i in range(DEPTH):
                copy_zt()
                fn(nodes[:, 0:NF], t1[:, 0:NF], ACT.Gelu_apprx_tanh)
            fn(st[:, 3, :], st[:, 2, :], ACT.Sqrt)
            for i in range(4):
                copy_zt()
            fn(t2[:, 0:NF], t1[:, 0:NF], ACT.Exp)
            fn(st[:, 3, :], st[:, 2, :], ACT.Ln)
            fn(st[:, 3, :], st[:, 2, :], ACT.Sqrt)

            act.wait_ge(nodes_ready, L3)

            def relu3(c, b, r):
                act.wait_ge(h3ps_ready, c + 1)
                act.wait_ge(w_free, c + DEPTH * C + 1)
                s.activation(h3[b % 2][0:EH, :], ps_h1[b % 2][0:EH, :], ACT.Relu).then_inc(h3_ready, 1)

            pipeline(act, [(relu3, 0)])
            fn(fs[:, 3, :], fs[:, 2, :], ACT.Sqrt)
            fn(st[:, 3, :], st[:, 2, :], ACT.Sqrt)

        @block.tensor
        def _(pe):
            pe.sem_inc(mv_free, 2)
            pe.wait_ge(loaded, 16 * (N_LOADS + 1))
            pe.wait_ge(consts_made, 2)

            def project(c, b, r):
                q = b % 2
                pe.wait_ge(a_xe, c + 1)
                if started(c, 1):
                    pe.wait_ge(a_xr, c)
                for h in range(2):
                    for k in range(TPC):
                        last = te.transpose(ps_x[:, h * CH + k * P:h * CH + (k + 1) * P],
                                            xe[q][:, k * W + h * HALF:k * W + (h + 1) * HALF], ident)
                last.then_inc(a_x, 1)
                pe.wait_ge(a_e16[q], turn(b, r) * 16 + 16)
                if started(c, 1):
                    pe.wait_ge(a_e2, c)
                for h in range(2):
                    last = te.matmul(ps_wa[:, h * CH:(h + 1) * CH], wa_sb[:, h * HALF:(h + 1) * HALF], e16[q], start=True, stop=True)
                last.then_inc(a_wa, 1)
                if started(c, 1):
                    pe.wait_ge(a_e1, c)
                for h in range(2):
                    last = te.matmul(ps_wm[:, h * CH:(h + 1) * CH], wm_sb[:, h * HALF:(h + 1) * HALF], e16[q], start=True, stop=True)
                last.then_inc(a_wm, 1)

            def rows(c, b, r):
                pe.wait_ge(a_q, c + 1)
                for k in range(TPC):
                    if started(c, 1) or k >= 2:
                        pe.wait_ge(a_rows, c * TPC + k - 1)
                    for n, part in enumerate((ss[b % 2], qq[b % 2])):
                        for h in range(2):
                            last = te.transpose(ps_rows[k % 2][:, n * W + h * HALF:n * W + (h + 1) * HALF],
                                                part[:, h * CH + k * P:h * CH + (k + 1) * P], ident)
                    last.then_inc(a_t, 1)

            pipeline(pe, [(project, 0), (rows, 2)])

            def zero_agg():
                te.matmul(ps_agg[:, 0:NF + HI], ones[:, :], zer[:, 0:NF + HI], start=True, stop=False, skip_group_check=True)

            def scatter_of(p, cols):
                def scatter(c, b, r):
                    pe.wait_ge(mv_ready, c + (p - 1) * C + 1)
                    for k in range(TPC):
                        last = te.matmul(ps_agg[:, 0:cols], oh[b % 2][:, k, :], mv[b % 2][:, k, 0:cols],
                                         start=False, stop=False, skip_group_check=True)
                    last.then_inc(mv_free, 1)
                return scatter

            def end_agg(p):
                te.matmul(ps_agg[:, 0:NF + HI], ones[:, :], zer[:, 0:NF + HI], start=False, stop=True,
                          skip_group_check=True).then_inc(agg_ready, 1)

            n_dense = 0

            def dense(wi):
                nonlocal n_dense
                n_dense += 1
                pe.wait_ge(z_ready, n_dense)
                for q in range(4):
                    last = te.transpose(ps_t[:, q * P:(q + 1) * P], nodes[:, q * P:(q + 1) * P], ident)
                last.then_inc(zt_ready, 1)
                pe.wait_ge(zt_copied, n_dense)
                for q in range(4):
                    last = te.matmul(ps_o[:, q * P:(q + 1) * P], zt_sb[:, q * P:(q + 1) * P], nw[:, wi, :], start=True, stop=True)
                last.then_inc(dense_ready, 1)

            for p in range(1, PHASES):
                pe.wait_ge(nodes_ready, p)
                zero_agg()

                def first(c, b, r):
                    pe.wait_ge(m6_loaded[b % 2], turn(b, r) * 16 + 16)
                    if started(c, 2):
                        pe.wait_ge(n_h1, c - 1)
                    te.matmul(ps_h1[b % 2], kw1_sb[:, :], m6[b % 2], start=True, stop=True).then_inc(n_h1ps, 1)

                def second(c, b, r):
                    pe.wait_ge(n_h1, c + 1)
                    if started(c, 1):
                        pe.wait_ge(n_h2, c)
                    te.matmul(ps_h2, kw2_sb[:, :], h1[b % 2], start=True, stop=True).then_inc(n_h2ps, 1)

                def weights(c, b, r, p=p):
                    if p == 1:
                        pe.wait_ge(n_h2, c + 1)
                    else:
                        pe.wait_ge(hb_loaded[b % 2], (turn(b, r) + (p - 2) * (C // 2) + 1) * 16)
                    pe.wait_ge(w_free, c + (p - 1) * C + 1)
                    for k in range(TPC):
                        o = ps_w[b % 2][:, k * W:(k + 1) * W]
                        te.matmul(o, hb[b % 2][:, k * P:(k + 1) * P], kw3_sb[:, :], start=True, stop=False)
                        last = te.matmul(o, ones_rows[:, :], kb3_rows[:, :], start=False, stop=True)
                    last.then_inc(w_ready, 1)

                def hidden3(c, b, r):
                    pe.wait_ge(m6_loaded[b % 2], (turn(b, r) + C // 2 + 1) * 16)
                    if started(c, 2):
                        pe.wait_ge(h3_ready, c - 1)
                    te.matmul(ps_h1[b % 2][0:EH, :], l3w1_sb[:, :], m6[b % 2], start=True, stop=True).then_inc(h3ps_ready, 1)

                def weights3(c, b, r):
                    pe.wait_ge(h3_ready, c + 1)
                    pe.wait_ge(w_free, c + DEPTH * C + 1)
                    for k in range(TPC):
                        last = te.matmul(ps_w[b % 2][:, k * W:(k + 1) * W], h3[b % 2][:, k * P:(k + 1) * P], l3w2_sb[:, :],
                                         start=True, stop=True)
                    last.then_inc(w_ready, 1)

                if p == 1:
                    pipeline(pe, [(first, 0), (second, 1), (weights, 2), (scatter_of(p, NF + HI), 3)])
                elif p < L2:
                    pipeline(pe, [(weights, 0), (scatter_of(p, NF), 1)])
                elif p < L3:
                    pipeline(pe, [(scatter_of(p, NF), 0)])
                else:
                    pe.wait_ge(bias_rows, 1)
                    pipeline(pe, [(hidden3, 0), (weights3, 1), (scatter_of(p, NF), 2)])
                end_agg(p)
                if p < L2:
                    dense(W_ROOT + p - 1)
                elif p == L2:
                    dense(W_1A)
                    dense(W_1B)
                elif p == L2 + 1:
                    dense(W_2A)
                    dense(W_2B)
                else:
                    for k in range(2):
                        pe.wait_ge(col_in, k + 1)
                        te.matmul(ps_o[:, 0:NF], ones[:, :], t1[:, 0:NF], start=True, stop=True).then_inc(col_out, 1)

        @block.vector
        def _(dve):
            dve.sem_inc(w_free, 2)

            def linker(chain, base):
                n = [0]

                def done(op, wait=True):
                    n[0] += 1
                    op.then_inc(chain, 1)
                    if wait:
                        dve.wait_ge(chain, base + n[0])
                return done

            done = linker(setup_chain, 0)
            v.memset(xn[:, :], 0.0).then_inc(consts_made, 1)
            done(v.memset(zer[:, :], 0.0), False)
            done(v.memset(nodes[:, :], 0.0), False)
            done(v.memset(ones[:, :], 1.0), False)
            done(v.memset(kb3_rows[:, :], 0.0), False)
            done(v.memset(ones_rows[:, :], 0.0), False)
            done(v.memset(st[:, :, :], 0.0))
            dve.wait_ge(loaded, 16 * (N_LOADS + 1))
            done(v.tensor_copy(kb3_h, kb3_f))
            done(v.tensor_tensor(kb3_r, kb3_f, kb3_h, ALU.subtract))
            done(v.tensor_copy(kb3_m, kb3_r))
            done(v.tensor_tensor(kb3_r, kb3_r, kb3_m, ALU.subtract))
            for row, part in ((0, kb3_h), (32, kb3_m), (64, kb3_r)):
                done(v.tensor_copy(kb3_rows[row:row + 1, :], part[row:row + 1, :]))
                done(v.memset(ones_rows[row:row + 1, :], 1.0))
            dve.sem_inc(consts_made, 1)
            dve.wait_ge(edges_loaded, 16 * 5)
            done(v.tensor_tensor(start, row_i, prv_i, ALU.not_equal))
            v.tensor_scalar(start, start, NEG, None, ALU.mult).then_inc(start_made, 1)
            done(v.tensor_tensor(end_f, dst_i, nxt_i, ALU.not_equal))
            done(v.tensor_scalar(end_f, end_f, -float(FAR), float(FAR), ALU.mult, ALU.add))
            done(v.tensor_tensor(end_row[:, :], end_f, dst_i, ALU.add))
            done(v.tensor_scalar(tmp_i, dst_i, 7, None, ALU.arith_shift_right))
            done(v.tensor_copy(dhi[:, :], tmp_i))
            done(v.tensor_scalar(tmp_i, dst_i, P - 1, None, ALU.bitwise_and))
            done(v.tensor_copy(dlo[:, :], tmp_i))
            done(v.memset(mm[:, :, 0:1], 0.0))
            dve.wait_ge(start_stored, 16)
            dve.sem_inc(setup_done, 1)

            def front(c, b, r):
                q = b % 2
                dve.wait_ge(a_wa, c + 1)
                dve.wait_ge(a_xr, c + 1)
                if started(c, 1):
                    dve.wait_ge(a_d, c)
                v.tensor_tensor(e2, ps_wa, xr[q], ALU.mult).then_inc(a_e2, 1)
                dve.wait_ge(a_neg[q], turn(b, r) * 16 + 16)
                if started(c, 1):
                    dve.wait_ge(a_carry, c)
                dve.wait_ge(a_e2, c + 1)
                for h in range(2):
                    last = v.tensor_tensor_scan(mm[:, h, 1:CH + 1], neg[q], e2[:, h * CH:(h + 1) * CH],
                                                mm[:, h, 0:1], ALU.add, ALU.max)
                last.then_inc(a_m, 1)
                dve.wait_ge(a_wm, c + 1)
                v.tensor_tensor(e1[q], ps_wm, xr[q], ALU.mult).then_inc(a_e1, 1)
                dve.wait_ge(a_m, c + 1)
                v.tensor_tensor(u.rearrange("p (h n) -> p h n", h=2), mm[:, :, 0:CH],
                                neg[q].unsqueeze(1).broadcast_to([P, 2, CH]), ALU.add).then_inc(a_u, 1)
                dve.wait_ge(a_u, c + 1)
                v.tensor_copy(mm[:, :, 0:1], mm[:, :, CH:CH + 1]).then_inc(a_carry, 1)
                if started(c, 2):
                    dve.wait_ge(a_ab, c - 1)
                v.tensor_tensor(dd[q], u, e2, ALU.subtract).then_inc(a_d, 1)

            def sums(c, b, r):
                q = b % 2
                dve.wait_ge(a_ab, c + 1)
                if started(c, 1):
                    dve.wait_ge(a_q, c)
                v.tensor_tensor(be, bb[q], e1[q], ALU.mult).then_inc(a_be, 1)
                if started(c, 2):
                    dve.wait_ge(a_t, (c - 1) * TPC)
                for dst_ap, src_ap in ((ss, bb[q]), (qq, be)):
                    for h in range(2):
                        at = slice(h * CH, (h + 1) * CH)
                        before = dst_ap[1 - q][:, (h + 1) * CH - 1:(h + 1) * CH] if started(c, 1) else 0.0
                        last = v.tensor_tensor_scan(dst_ap[q][:, at], aa[q][:, at], src_ap[:, at], before, ALU.mult, ALU.add)
                    if dst_ap is ss:
                        dve.wait_ge(a_be, c + 1)
                last.then_inc(a_q, 1)

            pipeline(dve, [(front, 0), (sums, 1)])

            done = linker(node_chain, 0)
            n_z = n_fn = n_col = 0

            def blocks(ap):
                return ap.rearrange("p (h f) -> p h f", f=F)

            def over_f(ap):
                return ap.unsqueeze(2).broadcast_to([P, HI, F])

            def over_h(ap):
                return ap.unsqueeze(1).broadcast_to([P, HI, F])

            N1, N2, ND = blocks(t1[:, 0:NF]), blocks(t2[:, 0:NF]), blocks(nodes[:, 0:NF])
            XN, AGG, DENSE = blocks(xn[:, 0:NF]), blocks(ps_agg[:, 0:NF]), blocks(ps_o[:, 0:NF])

            def function():
                nonlocal n_fn
                n_fn += 1
                dve.sem_inc(act_in, 1)
                dve.wait_ge(act_out, n_fn)

            def dense():
                nonlocal n_z
                n_z += 1
                dve.sem_inc(z_ready, 1)
                dve.wait_ge(dense_ready, n_z)

            def layernorm():
                done(v.tensor_reduce(st[:, 0, :], N1, X, ALU.add))
                done(v.tensor_scalar(st[:, 1, :], st[:, 0, :], 1.0 / F, None, ALU.mult))
                done(v.tensor_tensor(N1, N1, over_f(st[:, 1, :]), ALU.subtract))
                done(v.tensor_tensor(N2, N1, N1, ALU.mult))
                done(v.tensor_reduce(st[:, 0, :], N2, X, ALU.add))
                done(v.tensor_scalar(st[:, 2, :], st[:, 0, :], 1.0 / F, LN_EPS, ALU.mult, ALU.add))
                function()
                done(v.reciprocal(st[:, 4, :], st[:, 3, :]))
                done(v.tensor_tensor(ND, N1, over_f(st[:, 4, :]), ALU.mult))
                done(v.tensor_copy(xn[:, 0:NF], nodes[:, 0:NF]))

            dve.wait_ge(sums_loaded, 16)
            den, num = sq[:, :, 0:W], sq[:, :, W:2 * W]
            done(v.tensor_scalar(den, den, 1.0, None, ALU.max))
            done(v.reciprocal(den, den))
            done(v.tensor_tensor(num, num, den, ALU.mult))
            done(v.tensor_reduce(N2, num.rearrange("p h (i o) -> p h o i", i=F), X, ALU.add))
            done(v.tensor_tensor(N1, N2, XN, ALU.add))
            layernorm()
            done(v.tensor_tensor(ohi, iota[:, 0:HI].unsqueeze(1).broadcast_to([P, T, HI]),
                                 dhi[:, :].unsqueeze(2).broadcast_to([P, T, HI]), ALU.is_equal))
            dve.sem_inc(nodes_ready, 1)

            for p in range(1, PHASES):
                if p == L3:
                    for q in range(2):
                        done(v.memset(h3[q][EH:EH + 1, :], 1.0))
                    dve.sem_inc(bias_rows, 1)
                wp = p - 1 if p < L2 else DEPTH

                def message(c, b, r, p=p, wp=wp):
                    q = b % 2
                    dve.wait_ge(xg_loaded[b], (r + p * (C // 4) + 1) * (16 * TPC))
                    x_rows = xg[:, b, :].rearrange("p (k f) -> p k f", f=F)
                    if p not in (L2, L2 + 1):
                        dve.wait_ge(w_ready, c + wp * C + 1)
                        v.tensor_tensor(prod.rearrange("p (k i o) -> p k i o", i=F, o=F),
                                        ps_w[q].rearrange("p (k i o) -> p k i o", i=F, o=F),
                                        x_rows.unsqueeze(3).broadcast_to([P, TPC, F, F]), ALU.mult).then_inc(w_free, 1)
                    dve.wait_ge(mv_free, c + (p - 1) * C + 1)
                    v.tensor_tensor(oh[q], iota.unsqueeze(1).broadcast_to([P, TPC, P]),
                                    dlo[:, bass.ds(c * TPC, TPC)].unsqueeze(2).broadcast_to([P, TPC, P]), ALU.is_equal)
                    hot = ohi[:, bass.ds(c * TPC, TPC), :]
                    if p == 1:
                        v.tensor_copy(mv[q][:, :, NF:NF + HI], hot)
                    if p in (L2, L2 + 1):
                        sent = x_rows
                    else:
                        dve.wait_ge(w_free, c + wp * C + 3)
                        if started(c, 1):
                            dve.wait_ge(mv_ready, c + (p - 1) * C)
                        v.tensor_reduce(msg[:, :, :], prod.rearrange("p (k i o) -> p k o i", i=F, o=F), X, ALU.add)\
                         .then_inc(m_sum, 1)
                        dve.wait_ge(m_sum, c + wp * C + 1)
                        sent = msg[:, :, :]
                    v.tensor_tensor(mv[q][:, :, 0:NF].rearrange("p k (h f) -> p k h f", f=F),
                                    sent.unsqueeze(2).broadcast_to([P, TPC, HI, F]),
                                    hot.unsqueeze(3).broadcast_to([P, TPC, HI, F]), ALU.mult).then_inc(mv_ready, 1)

                pipeline(dve, [(message, 0)])
                dve.wait_ge(agg_ready, p)
                if p == 1:
                    deg = ps_agg[:, NF:NF + HI]
                    done(v.tensor_scalar(st[:, 0, :], deg, 1.0, None, ALU.max))
                    done(v.reciprocal(inv_deg1[:, :], st[:, 0, :]))
                    done(v.tensor_scalar(st[:, 1, :], deg, 0.0, None, ALU.is_gt))
                    done(v.tensor_tensor(inv_deg[:, :], st[:, 1, :], inv_deg1[:, :], ALU.mult))
                if p < L2:
                    done(v.tensor_tensor(N1, AGG, over_f(inv_deg[:, :]), ALU.mult))
                    dense()
                    done(v.tensor_tensor(N1, N1, DENSE, ALU.add))
                    done(v.tensor_tensor(N1, N1, over_h(nb[:, B_ROOT + p - 1, :]), ALU.add))
                    function()
                    if p == L2 - 1:
                        done(v.tensor_tensor(N1, XN, ND, ALU.add))
                        layernorm()
                elif p < L3:
                    q = p - L2
                    done(v.tensor_scalar(st[:, 0, 0:1], eps_sb[:, q:q + 1], 1.0, None, ALU.add))
                    done(v.tensor_scalar(t1[:, 0:NF], nodes[:, 0:NF], st[:, 0, 0:1], None, ALU.mult))
                    done(v.tensor_tensor(ND, N1, AGG, ALU.add))
                    dense()
                    done(v.tensor_tensor(N1, DENSE, over_h(nb[:, B_1A + 2 * q, :]), ALU.add))
                    done(v.tensor_scalar(nodes[:, 0:NF], t1[:, 0:NF], 0.0, None, ALU.max))
                    dense()
                    done(v.tensor_tensor(N1, DENSE, over_h(nb[:, B_1B + 2 * q, :]), ALU.add))
                    if q == 0:
                        done(v.tensor_scalar(nodes[:, 0:NF], t1[:, 0:NF], 0.0, None, ALU.max))
                    else:
                        done(v.tensor_reduce(st[:, 0, :], N1, X, ALU.max))
                        done(v.tensor_tensor(N1, N1, over_f(st[:, 0, :]), ALU.subtract))
                        function()
                        done(v.tensor_reduce(st[:, 2, :], N2, X, ALU.add))
                        function()
                        done(v.tensor_tensor(N1, N1, over_f(st[:, 3, :]), ALU.subtract))
                        done(v.tensor_tensor(N1, N1, XN, ALU.add))
                        layernorm()
                else:
                    done(v.tensor_tensor(N1, AGG, over_f(inv_deg1[:, :]), ALU.mult))
                    done(v.tensor_tensor(N1, N1, over_h(nb[:, B_BIAS, :]), ALU.add))
                    done(v.tensor_scalar(t1[:, 0:NF], t1[:, 0:NF], 0.0, None, ALU.max))
                    done(v.tensor_tensor(N1, N1, over_f(valid), ALU.mult))
                    for k in range(2):
                        dve.sem_inc(col_in, 1)
                        dve.wait_ge(col_out, k + 1)
                        done(v.tensor_reduce(fs[:, 0, :], ps_o[:, 0:NF].rearrange("p (h f) -> p f h", f=F), X, ALU.add))
                        if k == 0:
                            done(v.tensor_scalar(fs[:, 1, :], fs[:, 0, :], 1.0 / N, None, ALU.mult))
                            done(v.tensor_tensor(ND, N1, over_h(fs[:, 1, :]), ALU.subtract))
                            done(v.tensor_tensor(N2, ND, over_f(valid), ALU.mult))
                            done(v.tensor_tensor(N1, N2, N2, ALU.mult))
                    done(v.tensor_scalar(fs[:, 2, :], fs[:, 0, :], 1.0 / N, BN_EPS, ALU.mult, ALU.add))
                    function()
                    done(v.reciprocal(fs[:, 1, :], fs[:, 3, :]))
                    done(v.tensor_tensor(fs[:, 0, :], fs[:, 1, :], nb[:, B_GAMMA, :], ALU.mult))
                    done(v.tensor_tensor(N1, ND, over_h(fs[:, 0, :]), ALU.mult))
                    done(v.tensor_tensor(N1, N1, over_h(nb[:, B_BETA, :]), ALU.add))
                    done(v.tensor_tensor(N1, N1, XN, ALU.add))
                    layernorm()
                dve.sem_inc(nodes_ready, 1)


_OUT = ((N, F), 'float32')


def kernel(**inputs):
    import numpy as np
    import concourse.bacc as bacc
    from concourse.bass_utils import run_bass_kernel_spmd as run

    a = {k: np.asarray(val) for k, val in inputs.items()}

    def tiles(row):
        return np.ascontiguousarray(row.reshape(T, P).T)

    def with_bias(w, b):
        return np.concatenate([w, b[None, :]], axis=0)

    def padded(attr):
        d = attr.shape[1]
        o = np.zeros((d + 1, EP), np.float32)
        o[:d, :E] = attr.T
        o[d] = 1.0
        return o

    src = np.zeros(EP, np.int32)
    src[:E] = a['src']
    dst = np.full(EP, NPAD, np.int32)
    dst[:E] = a['dst']
    nxt = np.full(EP, -1, np.int32)
    nxt[:-1] = dst[1:]
    prv = np.full(EP, -1, np.int32)
    prv[1:] = dst[:-1]

    mats = list(a['L1_gnn_root_W']) + [a[f'L2_gnn_{k}'] for k in ('w1a', 'w1b', 'w2a', 'w2b')]
    node_w = np.zeros((P, NWM, P), np.float32)
    for n, m in enumerate(mats):
        for q in range(P // F):
            node_w[q * F:(q + 1) * F, n, q * F:(q + 1) * F] = m
    rows = list(a['L1_gnn_root_b']) + [a[f'L2_gnn_{k}'] for k in ('b1a', 'b1b', 'b2a', 'b2b')] + \
        [a[f'L3_gnn_{k}'] for k in ('bias', 'gamma', 'beta')]
    node_b = np.ascontiguousarray(np.broadcast_to(np.stack(rows), (P, NBR, F)))
    eps = np.ascontiguousarray(np.broadcast_to(np.stack([a['L2_gnn_eps1'], a['L2_gnn_eps2']]), (P, 2)))

    consts = np.zeros((P, NK), np.float32)
    consts[:, K_ID:K_ID + P] = np.eye(P)
    consts[:, K_IOTA:K_IOTA + P] = np.arange(P)
    consts[np.arange(P), K_SEL + np.arange(P) % F] = 1.0
    consts[:, K_VALID:K_VALID + HI] = (np.arange(HI)[None, :] * P + np.arange(P)[:, None]) < N

    data = {
        'x': a['x'], 'src_t': tiles(src), 'dst_t': tiles(dst), 'dst_next_t': tiles(nxt),
        'dst_row': dst.reshape(P, T), 'dst_prev_row': prv.reshape(P, T),
        'ef16': padded(a['edge_attr_16']), 'ef6': padded(a['edge_attr_6']),
        'w_attn': with_bias(a['L0_gnn_W_attn'], a['L0_gnn_b_attn']),
        'w_msg': with_bias(a['L0_gnn_W_msg'], a['L0_gnn_b_msg']),
        'kw1': with_bias(a['L1_gnn_kW1'], a['L1_gnn_kb1']),
        'kw2': a['L1_gnn_kW2'], 'kb2': a['L1_gnn_kb2'].reshape(KD, 1),
        'kw3': a['L1_gnn_kW3'], 'kb3': a['L1_gnn_kb3'],
        'l3w1': with_bias(a['L3_gnn_W1'], a['L3_gnn_b1']),
        'l3w2': with_bias(a['L3_gnn_W2'], a['L3_gnn_b2']),
        'node_w': node_w, 'node_b': node_b, 'eps': eps, 'consts': consts,
    }
    nc = bacc.Bacc("TRN2", target_bir_lowering=False, num_devices=1)
    arrays, args = {}, []
    for name, val in data.items():
        val = np.ascontiguousarray(val)
        arrays[f"in_{name}"] = val
        args.append(nc.dram_tensor(f"in_{name}", val.shape, mybir.dt.from_np(val.dtype), kind="ExternalInput").ap())
    out = nc.dram_tensor("out_nodes", _OUT[0], mybir.dt.from_np(np.dtype(_OUT[1])), kind="ExternalOutput").ap()
    gnn_resnorm(nc, *args, out)
    r = run(nc, [arrays], core_ids=[0])
    return r.results[0]["out_nodes"]
```

```python
import concourse.bass as bass
from concourse import mybir
from contextlib import ExitStack

N = 3125
E = 103125
F = 16
P = 128
HI = -(-N // P)
NF = HI * F
NPAD = HI * P
CH = 512
TPC = CH // P
C = 4 * (-(-E // (4 * CH)))
T = C * TPC
EP = C * CH
W = F * F
HALF = W // 2
KD = 128
EH = 64
D16, D6 = 16, 6
DEPTH = 4
LN_EPS = 1e-5
BN_EPS = 1e-5
NEG = -3.0e38
FAR = 1 << 20
CB = C // 2
LT = 2 * TPC
SW = 2 * W + 1
GROUP = 8
NG = CH // (GROUP * F)
PHASES = 1 + DEPTH + 2 + 1
L0, L1, L2, L3 = 0, 1, 1 + DEPTH, 3 + DEPTH

W_ROOT, W_1A, W_1B, W_2A, W_2B, NWM = 0, 4, 5, 6, 7, 8
B_ROOT, B_1A, B_1B, B_2A, B_2B, B_BIAS, B_GAMMA, B_BETA, NBR = 0, 4, 5, 6, 7, 8, 9, 10, 11
K_ID, K_IOTA, K_VALID, K_KEY, K_PART = 0, P, 2 * P, 2 * P + HI, 2 * P + HI + NG
NK = K_PART + 3
R6 = 9 * (D6 + 1)
E6 = (D6 + 1) * EP // P


def by_pe(p):
    if p == L0:
        return ()
    return (1, 3) if p in (L2, L2 + 1) else (3,)


def first_by_pe(p):
    return {L1: 3, L2: 0, L2 + 1: 0}.get(p, 2)


def tiles_by_pool(p, b):
    return first_by_pe(p) if b in by_pe(p) else TPC


def chunks_indexed(p):
    return 1 if p in (L2, L2 + 1) else 2


def rows_in(p, b, r):
    return (r + 1) * (16 * tiles_by_pool(p, b)) + 16 * (C // 4) * sum(tiles_by_pool(q, b) for q in range(p))


GB = [0] * PHASES
KB = [[0, 0] for _ in range(PHASES)]
for _p in range(1, PHASES):
    GB[_p] = GB[_p - 1] + len(by_pe(_p - 1)) * (C // 4)
    KB[_p] = [KB[_p - 1][_q] + (C // 4) * sum(_b // 2 == _q for _b in by_pe(_p - 1)) for _q in range(2)]


def nth(bs, b, r):
    return r * len(bs) + bs.index(b)



def pipeline(eng, stages, lead=4):
    for c in range(lead):
        for stage, lag in stages:
            if c >= lag:
                stage(c - lag, (c - lag) % 4, (c - lag) // 4)
    with eng.Fori(0, (C - lead) // 4) as i:
        for j in range(4):
            for stage, lag in stages:
                at = lead + j - lag
                stage(i * 4 + at, at % 4, i + at // 4)
    for c in range(C, C + max(lag for _, lag in stages)):
        for stage, lag in stages:
            if c - lag < C:
                stage(c - lag, (c - lag) % 4, (c - lag) // 4)


def turn(b, r):
    return r * 2 + b // 2


def started(c, n):
    return not isinstance(c, int) or c >= n


def gnn_resnorm(nc, x, src_t, dst_t, dst_next_t, dst_row, dst_next_row, src_row, dst_last, dst_after, edge_no, ef16, ef6, w_attn, w_msg,
                w1, kw2, kb2, kw3, kb3, l3w2, node_w, node_b, eps, consts, out):
    f32, bf16, f16, i32 = mybir.dt.float32, mybir.dt.bfloat16, mybir.dt.float16, mybir.dt.int32
    ALU, ACT, X = mybir.AluOpType, mybir.ActivationFunctionType, mybir.AxisListType.X
    v, s, g, te = nc.vector, nc.scalar, nc.gpsimd, nc.tensor

    tables = [x] + [nc.dram_tensor(f"node_table_{p}", (NPAD, F), f32, kind="Internal").ap()
                    for p in range(1, PHASES)]
    start_d = nc.dram_tensor("start_mask", (EP,), f32, kind="Internal").ap()
    sums_d = nc.dram_tensor("softmax_sums", (NPAD, SW), f32, kind="Internal").ap()
    dst_d = nc.dram_tensor("dst_half", (EP,), f16, kind="Internal").ap()
    key_d = nc.dram_tensor("src_key", (EP,), f16, kind="Internal").ap()
    y_d = {w: nc.dram_tensor(f"tile_sums_{w}", (EP + 1, w), f32, kind="Internal").ap() for w in (F, F + 1)}
    ef6_d = nc.dram_tensor("ef6_parts", (R6 // 3, EP), bf16, kind="Internal").ap()
    h2_d = nc.dram_tensor("edge_hidden", (C, P, CH), f32, kind="Internal").ap()

    ctx = ExitStack()
    with ctx:
        def sb(name, shape, dt=f32):
            return ctx.enter_context(nc.sbuf_tensor(name, shape, dt))

        def sem(name):
            return ctx.enter_context(nc.semaphore(name))

        def sems(name, n):
            return [sem(f"{name}_{k}") for k in range(n)]

        src_sb = sb("src_sb", [P, T], i32)
        dcol = sb("dcol", [P, T])
        end_row = sb("end_row", [P, T], i32)
        last_row = sb("last_row", [P, HI], i32)
        con = sb("con", [P, NK])
        ident, iota = con[:, K_ID:K_ID + P], con[:, K_IOTA:K_IOTA + P]
        valid, key_of = con[:, K_VALID:K_VALID + HI], con[:, K_KEY:K_KEY + NG]
        part_row = [con[0:R6, K_PART + k:K_PART + k + 1] for k in range(3)]
        nw = sb("nw", [P, NWM, P])
        nb = sb("nb", [P, NBR, F])
        eps_sb = sb("eps_sb", [P, 2])
        zer = sb("zer", [P, SW])
        ones = sb("ones", [P, P])
        wa_sb = sb("wa_sb", [P, W])
        wm_sb = sb("wm_sb", [P, W])
        w1_f = sb("w1_f", [R6, 2 * KD])
        w1_p = sb("w1_p", [R6, 3, 2 * KD], bf16)
        w1_sb = sb("w1_sb", [R6, 2 * KD], bf16)
        kw2_sb = sb("kw2_sb", [P, KD])
        kb2_sb = sb("kb2_sb", [P, 1])
        kw3_sb = sb("kw3_sb", [P, W])
        l3w2_sb = sb("l3w2_sb", [P, W])
        kb3_rows = sb("kb3_rows", [P, W], bf16)
        ones_rows = sb("ones_rows", [P, P], bf16)
        xn = sb("xn", [P, CH])
        nodes = sb("nodes", [P, CH])
        zt_sb = sb("zt_sb", [P, CH])
        t1 = sb("t1", [P, CH])
        t2 = sb("t2", [P, CH])
        st = sb("st", [P, 6, HI])
        fs = sb("fs", [P, 4, F])
        inv_deg = sb("inv_deg", [P, HI])
        inv_deg1 = sb("inv_deg1", [P, HI])
        idx = sb("idx", [P, 4, TPC], i32)
        idx_end = sb("idx_end", [P, 2, TPC], i32)
        xg = sb("xg", [P, 4, TPC * F])
        msg = sb("msg", [P, 2, TPC, F + 1])
        last_sb = sb("last_sb", [CB, 2, LT], i32)

        arena = sb("arena", [P, 30 * 2 * CH])

        def area(k, n=2 * CH):
            return arena[:, k * 2 * CH:k * 2 * CH + n]

        def halves(k, rows=P):
            return [arena[0:rows, k * 2 * CH + q * CH:k * 2 * CH + (q + 1) * CH] for q in range(2)]

        dst_i, nxt_i, row_i, nxr_i, tmp_i, src_i = (area(k, T).bitcast(i32) for k in range(6))
        start, end_f = area(6, T), area(7, T)
        drow_h = area(8, T // 2).bitcast(f16)
        kb3_f, kb3_r = area(9, W), area(10, W)
        kb3_h, kb3_m = (area(k, W // 2).bitcast(bf16) for k in (11, 12))
        key_h = area(13, T // 2).bitcast(f16)
        ef_f = arena[:, 14 * 1024:14 * 1024 + E6]
        ef_p = [arena[:, (20 + 3 * k) * 1024:(20 + 3 * k) * 1024 + E6 // 2].bitcast(bf16) for k in range(3)]
        e16, neg = halves(0), halves(1)
        xr = [area(2), area(3)]
        e2 = area(4)
        e1 = [area(6), area(7)]
        dd = [area(8), area(9)]
        rel = [area(10), area(11)]
        aa, bb = [area(12), area(13)], [area(14), area(15)]
        be = area(16)
        ss, qq = [area(17), area(18)], [area(19), area(20)]
        xe = [area(21), area(22)]
        rows_sq = arena[:, 23 * 1024:23 * 1024 + 2 * TPC * SW].rearrange("p (q k c) -> p q k c", q=2, k=TPC)
        mm = arena[:, 28 * 1024 - 512:28 * 1024 - 512 + 2 * (CH + 1)].rearrange("p (h n) -> p h n", h=2)
        e_no = area(29, T)
        sq = arena[:, 0:HI * SW].rearrange("p (h c) -> p h c", h=HI)
        hb = halves(0) + halves(29)
        prod = area(1)
        m6 = [h[:, 0:CH // 2].bitcast(bf16) for h in halves(2, R6)]
        h1 = halves(3)
        h3 = halves(4)
        same = [h.rearrange("p (k n) -> p k n", k=TPC) for h in halves(5)]
        drow = [area(k, CH).bitcast(f16) for k in (6, 7)]
        keys = [arena[:, (8 + q) * 1024:(8 + q) * 1024 + CH // 2].bitcast(f16) for q in range(2)]
        hot = [area(k).bitcast(bf16).rearrange("p (g n) -> p g n", g=NG) for k in (10, 27)]
        picked = area(11, CH)
        ysum = [h[:, 0:TPC * (F + 1)] for h in halves(12)]
        xs = [arena[:, 13 * 1024 + k * CH // 2:13 * 1024 + (k + 1) * CH // 2].bitcast(bf16) for k in range(3)]
        xs_r = area(14, CH)
        yg, agg = (h[:, 0:HI * (F + 1)] for h in halves(15))
        lrow = arena[0:CB, 16 * 1024:16 * 1024 + LT * (F + 1)]
        lmv = arena[0:CB, 17 * 1024:17 * 1024 + LT * HI * (F + 1)]
        sel8 = arena[:, 21 * 1024:21 * 1024 + T * GROUP // 2].bitcast(bf16).rearrange("p (t h) -> p t h", h=GROUP)
        l_lo = arena[0:CB, 25 * 1024:25 * 1024 + LT * P].rearrange("p (t n) -> p t n", t=LT)
        l_hi = arena[0:CB, 26 * 1024:26 * 1024 + LT * HI].rearrange("p (t h) -> p t h", t=LT)
        l_f = arena[0:CB, 26 * 1024 + 512:26 * 1024 + 512 + 4 * LT].rearrange("p (n t) -> p n t", n=4)
        l_i = arena[0:CB, 26 * 1024 + 600:26 * 1024 + 600 + LT].bitcast(i32)
        s_i, s_f = area(27, T).bitcast(i32), area(28, T)

        psum = ctx.enter_context(nc.psum_tensor("psum", [P, 8 * CH], f32))

        def bank(k, n=CH):
            return psum[:, k * CH:k * CH + n]

        ps_x, ps_wa, ps_wm = bank(0, 2 * CH), bank(2, 2 * CH), bank(4, 2 * CH)
        ps_rows = [bank(6), bank(7)]
        ps_w = [bank(0, 2 * CH), bank(2, 2 * CH)]
        ps_h1, ps_h2, ps_y = bank(4), bank(5), bank(7, TPC * (F + 1))

        def ps_g(p, b):
            return bank(0) if p in (L2, L2 + 1) and b // 2 == 0 else bank(6)

        ps_t, ps_o = bank(4), bank(5)
        ps_agg = bank(7)

        loaded = sem("loaded")
        edges_loaded = sem("edges_loaded")
        consts_made = sem("consts_made")
        start_made = sem("start_made")
        start_stored = sem("start_stored")
        setup_chain = sem("setup_chain")
        setup_done = sem("setup_done")
        idx_ready = sem("idx_ready")
        xg_loaded = sems("xg_loaded", 4)
        drow_loaded, key_loaded = sems("drow_loaded", 2), sems("key_loaded", 2)
        xs_ready = sem("xs_ready")
        hot_ready, picks_ready, picked_ready, pick_done = sem("hot_ready"), sem("picks_ready"), sem("picked_ready"), sem("pick_done")
        msg_ready = sem("msg_ready")
        y_ready, y_copied = sem("y_ready"), sem("y_copied")
        y_stored = sems("y_stored", 2)
        zero_rows_stored = sem("zero_rows_stored")
        last_loaded, lmv_ready = sem("last_loaded"), sem("lmv_ready")
        yg_loaded, agg_ready = sem("yg_loaded"), sem("agg_ready")
        sums_zeroed = sem("sums_zeroed")
        a_e16 = sems("a_e16_loaded", 2)
        a_neg = sems("a_neg_loaded", 2)
        a_xe, a_x, a_xr = sem("a_xe_ready"), sem("a_x_ready"), sem("a_xr_ready")
        a_wa, a_wm = sem("a_wa_ready"), sem("a_wm_ready")
        a_e2, a_e1, a_m = sem("a_e2_ready"), sem("a_e1_ready"), sem("a_m_ready")
        a_carry, a_d = sem("a_carry_ready"), sem("a_d_ready")
        a_rel, a_ab = sem("a_rel_ready"), sem("a_ab_ready")
        a_be, a_q = sem("a_be_ready"), sem("a_q_ready")
        a_t, a_rows = sem("a_transposed"), sem("a_rows_ready")
        a_end = sem("a_end_index_ready")
        a_sent = sems("a_sums_sent", 2)
        SPLIT = 5
        sums_loaded = sems("sums_loaded", SPLIT)
        ef_loaded, ef_made, ef_stored = sem("ef_loaded"), sem("ef_made"), sem("ef_stored")
        m6_loaded = sems("m6_loaded", 2)
        n_h1ps, n_h1, n_h2ps, n_h2 = sem("n_h1ps"), sem("n_h1"), sem("n_h2ps"), sem("n_h2")
        n_stored = sems("n_h2_stored", 2)
        hb_loaded = sems("hb_loaded", 4)
        h3ps_ready, h3_ready = sem("h3ps_ready"), sem("h3_ready")
        w_ready = sem("w_ready")
        w_free = sem("w_free")
        bias_rows = sem("bias_rows")
        z_ready, zt_ready, zt_copied, dense_ready = sem("z_ready"), sem("zt_ready"), sem("zt_copied"), sem("dense_ready")
        col_in, col_out = sem("col_in"), sem("col_out")
        act_in, act_out = sem("act_in"), sem("act_out")
        node_chain = sem("node_chain")
        nodes_ready = sem("nodes_ready")
        table_stored = sem("table_stored")
        out_stored = sem("out_stored")

        N_LOADS = 13
        block = ctx.enter_context(nc.Block())

        @block.sync
        def _(sp):
            for dst_ap, src_ap in ((dst_i, dst_t), (nxt_i, dst_next_t), (row_i, dst_row),
                                   (nxr_i, dst_next_row), (src_sb[:, :], src_t), (src_i, src_row),
                                   (last_sb[:, 0, :], dst_last), (last_sb[:, 1, :], dst_after), (e_no, edge_no)):
                sp.dma_start(dst_ap, src_ap).then_inc(edges_loaded, 16)
            sp.dma_start(w1_f[:, :], w1).then_inc(loaded, 16)
            sp.dma_start(kw2_sb[:, :], kw2).then_inc(loaded, 16)
            sp.dma_start(kb2_sb[:, :], kb2).then_inc(loaded, 16)
            sp.dma_start(con[:, :], consts).then_inc(loaded, 16)
            sp.dma_start(kw3_sb[:, :], kw3).then_inc(loaded, 16)
            sp.dma_start(kb3_f, kb3.partition_broadcast(P)).then_inc(loaded, 16)
            sp.dma_start(wa_sb[:, :], w_attn).then_inc(loaded, 16)
            sp.dma_start(wm_sb[:, :], w_msg).then_inc(loaded, 16)
            sp.dma_start(l3w2_sb[:, :], l3w2).then_inc(loaded, 16)
            sp.dma_start(nw[:, :, :], node_w).then_inc(loaded, 16)
            sp.dma_start(nb[:, :, :], node_b).then_inc(loaded, 16)
            sp.dma_start(eps_sb[:, :], eps).then_inc(loaded, 16)
            sp.wait_ge(consts_made, 1)
            sp.dma_start(xn[:, 0:(HI - 1) * F].rearrange("p (h f) -> p h f", f=F),
                         x[0:(HI - 1) * P, :].rearrange("(h p) f -> p h f", p=P)).then_inc(loaded, 16)
            sp.dma_start(xn[0:N - (HI - 1) * P, (HI - 1) * F:NF], x[(HI - 1) * P:N, :]).then_inc(loaded, 16)

            sp.wait_ge(start_made, 3)
            for dst_ap, src_ap in ((start_d, start), (dst_d, drow_h), (key_d, key_h)):
                sp.dma_start(dst_ap.rearrange("(p t) -> p t", p=P), src_ap).then_inc(start_stored, 16)
            sp.wait_ge(setup_chain, 2)
            sp.dma_start(sums_d.rearrange("(h p) c -> p h c", p=P),
                         zer[:, :].unsqueeze(1).broadcast_to([P, HI, SW])).then_inc(sums_zeroed, 16)
            for w in (F, F + 1):
                sp.dma_start(y_d[w][EP:EP + 1, :], zer[0:1, 0:w]).then_inc(zero_rows_stored, 16)

            sp.wait_ge(setup_done, 1)

            def load_l0(c, b, r):
                q = b % 2
                if started(c, 2):
                    sp.wait_ge(a_e1, c - 1)
                sp.dma_start(e16[q][0:D16 + 1, :], ef16[:, bass.ds(c * CH, CH)]).then_inc(a_e16[q], 16)
                if started(c, 2):
                    sp.wait_ge(a_m, c - 1)
                sp.dma_start(neg[q], start_d[bass.ds(c * CH, CH)].partition_broadcast(P)).then_inc(a_neg[q], 16)

            pipeline(sp, [(load_l0, 0)])
            for q in range(2):
                sp.wait_ge(a_sent[q], 16 * TPC * (C // 2))
            sp.dma_start(ef_f, ef6.rearrange("r e -> (r e)").rearrange("(p n) -> p n", p=P)).then_inc(ef_loaded, 16)
            for k in range(SPLIT):
                at = slice(k * HI // SPLIT, (k + 1) * HI // SPLIT)
                sp.dma_start(sq[:, at, :], sums_d.rearrange("(h p) c -> p h c", p=P)[:, at, :]).then_inc(sums_loaded[k], 16)
            sp.wait_ge(ef_made, 1)
            for k in range(3):
                sp.dma_start(ef6_d[k * (D6 + 1):(k + 1) * (D6 + 1), :].rearrange("r e -> (r e)").rearrange("(p n) -> p n", p=P),
                             ef_p[k]).then_inc(ef_stored, 16)

            for p in range(1, PHASES):
                sp.wait_ge(nodes_ready, p)
                sp.dma_start(tables[p].rearrange("(h p) f -> p h f", p=P),
                             nodes[:, 0:NF].rearrange("p (h f) -> p h f", f=F)).then_inc(table_stored, 16)

                def load_m6(c, b, r, p=p):
                    q = b % 2
                    if started(c, 2):
                        sp.wait_ge(n_h1 if p == 1 else h3_ready, c - 1)
                    for k in range(3):
                        sp.dma_start(m6[q][k * (R6 // 3):(k + 1) * (R6 // 3), :], ef6_d[:, bass.ds(c * CH, CH)])\
                          .then_inc(m6_loaded[q], 16)

                def load_hidden(c, b, r, p=p):
                    sp.wait_ge(w_ready, c + (p - 1) * C - 3)
                    sp.dma_start(hb[b], h2_d[bass.ds(c, 1), :, :].rearrange("o p n -> (o p) n")).then_inc(hb_loaded[b], 16)

                def load_dst(c, b, r, p=p):
                    idx_c, q = c + (p - 1) * C, b // 2
                    if b % 2 == 0:
                        if started(c, 4):
                            sp.wait_ge(msg_ready, idx_c - 2)
                            sp.nop(nofuse=True)
                        sp.dma_start(drow[q], dst_d[bass.ds(c * CH, 2 * CH)].partition_broadcast(P)).then_inc(drow_loaded[q], 16)

                def load_keys(c, b, r, p=p):
                    q = b // 2
                    if b in by_pe(p):
                        if started(c, 4):
                            sp.wait_ge(hot_ready, nth(by_pe(p), b, r) + GB[p] + 1 - len(by_pe(p)))
                            sp.nop(nofuse=True)
                        sp.dma_start(keys[q], key_d[bass.ds(c * CH, CH)].partition_broadcast(P)).then_inc(key_loaded[q], 16)

                if p == 1:
                    stages = [(load_m6, 0), (load_keys, 0), (load_dst, 2)]
                elif p < L2:
                    stages = [(load_hidden, 0), (load_keys, 0), (load_dst, 2)]
                elif p < L3:
                    stages = [(load_keys, 0), (load_dst, 2)]
                else:
                    stages = [(load_m6, 0), (load_keys, 0), (load_dst, 2)]
                pipeline(sp, stages)
                if p == 1:
                    for q in range(2):
                        sp.wait_ge(n_stored[q], 16 * (C // 2))
                for q in range(2):
                    sp.wait_ge(y_stored[q], 16 * (C // 2) * p)
                w = F + 1 if p == 1 else F
                lasts = y_d[w][0:EP, :].rearrange("(n p r) f -> p n r f", n=2, r=CH)[:, :, CH - TPC:CH, :]
                for n in range(2):
                    sp.dma_start(lrow[:, n * TPC * w:(n + 1) * TPC * w],
                                 lasts[:, n, :, :].rearrange("p r f -> p (r f)")).then_inc(last_loaded, 16)
            sp.wait_ge(nodes_ready, PHASES)
            sp.dma_start(out[0:(HI - 1) * P, :].rearrange("(h p) f -> p h f", p=P),
                         nodes[:, 0:(HI - 1) * F].rearrange("p (h f) -> p h f", f=F)).then_inc(out_stored, 16)
            sp.dma_start(out[(HI - 1) * P:N, :], nodes[0:N - (HI - 1) * P, (HI - 1) * F:NF]).then_inc(out_stored, 16)
            sp.wait_ge(out_stored, 32)

        @block.gpsimd
        def _(pool):
            pool.wait_ge(edges_loaded, 16 * 9)
            pool.wait_ge(setup_done, 1)
            for p in range(PHASES):
                if p:
                    pool.wait_ge(table_stored, 16 * p)

                def gather(c, b, r, p=p):
                    n = chunks_indexed(p)
                    if b % n == 0:
                        if p == L0 and started(c, 4):
                            pool.wait_ge(a_xe, c - 4 + n)
                        elif p in (L2, L2 + 1) and started(c, 4):
                            pool.wait_ge(y_ready, c + (p - 1) * C - 4 + n)
                        elif started(c, 4):
                            pool.wait_ge(w_free, c + (p - 1 if p < L2 else DEPTH) * C - 2 + n)
                        pool.nop(nofuse=True)
                        g.tensor_copy(idx[:, b:b + n, :].rearrange("p b k -> p (b k)"),
                                      src_sb[:, bass.ds(c * TPC, n * TPC)]).then_inc(idx_ready, 1)
                        copies = sum(C // chunks_indexed(q) for q in range(p))
                        pool.wait_ge(idx_ready, r * (4 // n) + b // n + copies + 1)
                        pool.nop(nofuse=True)
                    for k in range(tiles_by_pool(p, b)):
                        pool.indirect_dma_start(
                            xg[:, b, k * F:(k + 1) * F], None, tables[p],
                            bass.IndirectOffsetOnAxis(ap=idx[:, b, k:k + 1], axis=0)).then_inc(xg_loaded[b], 16)

                def send_sums(c, b, r):
                    q = b % 2
                    if started(c, 2):
                        pool.wait_ge(a_sent[q], turn(b, r) * (16 * TPC))
                    pool.nop(nofuse=True)
                    g.tensor_copy(idx_end[:, q, :], end_row[:, bass.ds(c * TPC, TPC)]).then_inc(a_end, 1)
                    pool.wait_ge(a_end, c + 1)
                    pool.wait_ge(a_rows, c * TPC + TPC)
                    pool.nop(nofuse=True)
                    for k in range(TPC):
                        pool.indirect_dma_start(
                            sums_d, bass.IndirectOffsetOnAxis(ap=idx_end[:, q, k:k + 1], axis=0), rows_sq[:, q, k, :], None,
                            bounds_check=NPAD - 1, oob_is_err=False).then_inc(a_sent[q], 16)

                if p == L0:
                    pool.wait_ge(sums_zeroed, 16)
                    pipeline(pool, [(gather, 0), (send_sums, 6)], lead=8)
                else:
                    pipeline(pool, [(gather, 0)])
                    for q in range(2):
                        pool.wait_ge(y_stored[q], 16 * (C // 2) * p)
                    pool.wait_ge(zero_rows_stored, 32)
                    pool.wait_ge(nodes_ready, 1)
                    w = F + 1 if p == 1 else F
                    for h in range(HI):
                        pool.indirect_dma_start(
                            yg[:, h * w:(h + 1) * w], None, y_d[w],
                            bass.IndirectOffsetOnAxis(ap=last_row[:, h:h + 1], axis=0)).then_inc(yg_loaded, 16)

        @block.scalar
        def _(act):
            act.wait_ge(loaded, 16 * (N_LOADS + 1))

            def expand(c, b, r):
                act.wait_ge(xg_loaded[b], (r + 1) * (16 * TPC))
                if started(c, 2):
                    act.wait_ge(a_x, c - 1)
                s.copy(xe[b % 2].rearrange("p (k i o) -> p k i o", i=F, o=F),
                       xg[:, b, :].rearrange("p (k i) -> p k i", i=F).unsqueeze(3).broadcast_to([P, TPC, F, F]))\
                 .then_inc(a_xe, 1)

            def copy_x(c, b, r):
                act.wait_ge(a_x, c + 1)
                if started(c, 2):
                    act.wait_ge(a_e1, c - 1)
                s.copy(xr[b % 2], ps_x).then_inc(a_xr, 1)

            def exps(c, b, r):
                q = b % 2
                act.wait_ge(a_d, c + 1)
                if started(c, 1):
                    act.wait_ge(a_ab, c)
                s.activation(rel[0], dd[q], ACT.Relu).then_inc(a_rel, 1)
                s.activation(rel[1], dd[q], ACT.Relu, scale=-1.0).then_inc(a_rel, 1)
                if started(c, 2):
                    act.wait_ge(a_q, c - 1)
                act.wait_ge(a_rel, c * 2 + 1)
                s.activation(bb[q], rel[0], ACT.Exp, scale=-1.0)
                act.wait_ge(a_rel, c * 2 + 2)
                s.activation(aa[q], rel[1], ACT.Exp, scale=-1.0).then_inc(a_ab, 1)

            def copy_rows(c, b, r):
                q = b % 2
                if started(c, 2):
                    act.wait_ge(a_sent[q], turn(b, r) * (16 * TPC))
                s.copy(rows_sq[:, q, :, 2 * W:SW], e_no[:, bass.ds(c * TPC, TPC)].unsqueeze(2))
                for k in range(TPC):
                    act.wait_ge(a_t, c * TPC + k + 1)
                    s.copy(rows_sq[:, q, k, 0:2 * W], ps_rows[k % 2]).then_inc(a_rows, 1)

            pipeline(act, [(expand, 0), (copy_x, 1), (exps, 2), (copy_rows, 3)], lead=8)

            n_copy = n_fn = 0

            def copy_zt():
                nonlocal n_copy
                n_copy += 1
                act.wait_ge(zt_ready, n_copy)
                s.copy(zt_sb[:, :], ps_t).then_inc(zt_copied, 1)

            def fn(dst_ap, src_ap, func):
                nonlocal n_fn
                n_fn += 1
                act.wait_ge(act_in, n_fn)
                s.activation(dst_ap, src_ap, func).then_inc(act_out, 1)

            fn(st[:, 3, :], st[:, 2, :], ACT.Sqrt)

            def gelu1(c, b, r):
                act.wait_ge(n_h1ps, c + 1)
                if started(c, 2):
                    act.wait_ge(n_h2ps, c - 1)
                s.activation(h1[b % 2], ps_h1, ACT.Gelu_apprx_tanh).then_inc(n_h1, 1)

            def gelu2(c, b, r):
                act.wait_ge(n_h2ps, c + 1)
                if started(c, 2):
                    act.wait_ge(n_stored[b % 2], turn(b, r) * 16)
                    act.wait_ge(w_free, c + 1)
                s.activation(hb[b % 2], ps_h2, ACT.Gelu_apprx_tanh, bias=kb2_sb[:, 0:1]).then_inc(n_h2, 1)

            def copy_y(p):
                def copy(c, b, r):
                    q, w = b % 2, F + 1 if p == 1 else F
                    act.wait_ge(y_ready, c + (p - 1) * C + 1)
                    if started(c, 2):
                        act.wait_ge(y_stored[q], (turn(b, r) + (p - 1) * (C // 2)) * 16)
                    s.copy(ysum[q][:, 0:TPC * w], ps_y[:, 0:TPC * w]).then_inc(y_copied, 1)
                return copy

            def store_h2(c, b, r):
                act.wait_ge(n_h2, c + 1)
                act.dma_start(h2_d[bass.ds(c, 1), :, :].rearrange("o p n -> (o p) n"), hb[b % 2]).then_inc(n_stored[b % 2], 16)

            def store_y(p):
                def store(c, b, r):
                    w = F + 1 if p == 1 else F
                    act.wait_ge(y_copied, c + (p - 1) * C + 1)
                    act.dma_start(y_d[w][bass.ds(c * CH, CH), :].rearrange("(p k) f -> p (k f)", k=TPC),
                                  ysum[b % 2][:, 0:TPC * w]).then_inc(y_stored[b % 2], 16)
                return store

            for i in range(DEPTH):
                act.wait_ge(nodes_ready, i + 1)
                if i == 0:
                    pipeline(act, [(gelu1, 0), (gelu2, 1), (store_h2, 2), (copy_y(1), 4), (store_y(1), 5)], lead=8)
                else:
                    pipeline(act, [(copy_y(i + 1), 0), (store_y(i + 1), 0)])
                copy_zt()
                fn(nodes[:, 0:NF], t1[:, 0:NF], ACT.Gelu_apprx_tanh)
            fn(st[:, 3, :], st[:, 2, :], ACT.Sqrt)
            for p in (L2, L2 + 1):
                act.wait_ge(nodes_ready, p)
                pipeline(act, [(copy_y(p), 0), (store_y(p), 0)])
                copy_zt()
                copy_zt()
            fn(t2[:, 0:NF], t1[:, 0:NF], ACT.Exp)
            fn(st[:, 3, :], st[:, 2, :], ACT.Ln)
            fn(st[:, 3, :], st[:, 2, :], ACT.Sqrt)

            act.wait_ge(nodes_ready, L3)

            def relu3(c, b, r):
                act.wait_ge(h3ps_ready, c + 1)
                if started(c, 2):
                    act.wait_ge(w_ready, c + DEPTH * C - 1)
                s.activation(h3[b % 2][0:EH, :], ps_h1[0:EH, :], ACT.Relu).then_inc(h3_ready, 1)

            pipeline(act, [(relu3, 0), (copy_y(L3), 3), (store_y(L3), 3)])
            fn(fs[:, 3, :], fs[:, 2, :], ACT.Sqrt)
            fn(st[:, 3, :], st[:, 2, :], ACT.Sqrt)

        @block.tensor
        def _(pe):
            pe.wait_ge(loaded, 16 * (N_LOADS + 1))
            pe.wait_ge(consts_made, 2)

            def project(c, b, r):
                q = b % 2
                pe.wait_ge(a_xe, c + 1)
                if started(c, 1):
                    pe.wait_ge(a_xr, c)
                for h in range(2):
                    for k in range(TPC):
                        last = te.transpose(ps_x[:, h * CH + k * P:h * CH + (k + 1) * P],
                                            xe[q][:, k * W + h * HALF:k * W + (h + 1) * HALF], ident)
                last.then_inc(a_x, 1)
                pe.wait_ge(a_e16[q], turn(b, r) * 16 + 16)
                if started(c, 1):
                    pe.wait_ge(a_e2, c)
                for h in range(2):
                    last = te.matmul(ps_wa[:, h * CH:(h + 1) * CH], wa_sb[:, h * HALF:(h + 1) * HALF], e16[q], start=True, stop=True)
                last.then_inc(a_wa, 1)
                if started(c, 1):
                    pe.wait_ge(a_e1, c)
                for h in range(2):
                    last = te.matmul(ps_wm[:, h * CH:(h + 1) * CH], wm_sb[:, h * HALF:(h + 1) * HALF], e16[q], start=True, stop=True)
                last.then_inc(a_wm, 1)

            def rows(c, b, r):
                pe.wait_ge(a_q, c + 1)
                for k in range(TPC):
                    if started(c, 1) or k >= 2:
                        pe.wait_ge(a_rows, c * TPC + k - 1)
                    for n, part in enumerate((ss[b % 2], qq[b % 2])):
                        for h in range(2):
                            last = te.transpose(ps_rows[k % 2][:, n * W + h * HALF:n * W + (h + 1) * HALF],
                                                part[:, h * CH + k * P:h * CH + (k + 1) * P], ident)
                    last.then_inc(a_t, 1)

            pipeline(pe, [(project, 0), (rows, 2)])

            n_dense = 0

            def dense(wi):
                nonlocal n_dense
                n_dense += 1
                pe.wait_ge(z_ready, n_dense)
                for q in range(4):
                    last = te.transpose(ps_t[:, q * P:(q + 1) * P], nodes[:, q * P:(q + 1) * P], ident)
                last.then_inc(zt_ready, 1)
                pe.wait_ge(zt_copied, n_dense)
                for q in range(4):
                    last = te.matmul(ps_o[:, q * P:(q + 1) * P], zt_sb[:, q * P:(q + 1) * P], nw[:, wi, :], start=True, stop=True)
                last.then_inc(dense_ready, 1)

            for p in range(1, PHASES):
                pe.wait_ge(nodes_ready, p)

                def gather_of(p):
                    def gather(c, b, r):
                        if b not in by_pe(p):
                            return
                        n = nth(by_pe(p), b, r) + GB[p]
                        pe.wait_ge(hot_ready, n + 1)
                        if started(c, 4) or GB[p]:
                            pe.wait_ge(picked_ready, n + 1 - len(by_pe(p)))
                        for k in range(first_by_pe(p), TPC):
                            for j in range(NG):
                                for part in range(3):
                                    last = te.matmul(ps_g(p, b)[:, k * P:(k + 1) * P], hot[b // 2][:, j, k * P:(k + 1) * P],
                                                     xs[part][:, j * P:(j + 1) * P],
                                                     start=(j == 0 and part == 0), stop=(j == NG - 1 and part == 2))
                        last.then_inc(picks_ready, 1)
                    return gather

                def tile_sums(c, b, r, p=p):
                    w = F + 1 if p == 1 else F
                    pe.wait_ge(msg_ready, c + (p - 1) * C + 1)
                    if p in (L2, L2 + 1):
                        pe.wait_ge(xg_loaded[b], rows_in(p, b, r))
                    if started(c, 1):
                        pe.wait_ge(y_copied, c + (p - 1) * C)
                    for k in range(TPC):
                        sent = xg[:, b, k * F:(k + 1) * F] if p in (L2, L2 + 1) else msg[:, b % 2, k, 0:w]
                        last = te.matmul(ps_y[:, k * w:(k + 1) * w], same[b % 2][:, k, :], sent, start=True, stop=True)
                    last.then_inc(y_ready, 1)

                def first(c, b, r):
                    pe.wait_ge(m6_loaded[b % 2], turn(b, r) * 48 + 48)
                    if started(c, 1):
                        pe.wait_ge(n_h1, c)
                    te.matmul(ps_h1, w1_sb[:, 0:KD], m6[b % 2], start=True, stop=True).then_inc(n_h1ps, 1)

                def second(c, b, r):
                    pe.wait_ge(n_h1, c + 1)
                    if started(c, 1):
                        pe.wait_ge(n_h2, c)
                    te.matmul(ps_h2, kw2_sb[:, :], h1[b % 2], start=True, stop=True).then_inc(n_h2ps, 1)

                def weights(c, b, r, p=p):
                    if p == 1:
                        pe.wait_ge(n_h2, c + 1)
                    else:
                        pe.wait_ge(hb_loaded[b], (r + (p - 2) * (C // 4) + 1) * 16)
                    pe.wait_ge(w_free, c + (p - 1) * C + 1)
                    for k in range(TPC):
                        o = ps_w[b % 2][:, k * W:(k + 1) * W]
                        te.matmul(o, hb[b % 2 if p == 1 else b][:, k * P:(k + 1) * P], kw3_sb[:, :], start=True, stop=False)
                        last = te.matmul(o, ones_rows[:, :], kb3_rows[:, :], start=False, stop=True)
                    last.then_inc(w_ready, 1)

                def hidden3(c, b, r):
                    pe.wait_ge(m6_loaded[b % 2], (turn(b, r) + C // 2 + 1) * 48)
                    if started(c, 1):
                        pe.wait_ge(h3_ready, c)
                    te.matmul(ps_h1, w1_sb[:, KD:2 * KD], m6[b % 2], start=True, stop=True).then_inc(h3ps_ready, 1)

                def weights3(c, b, r):
                    pe.wait_ge(h3_ready, c + 1)
                    pe.wait_ge(w_free, c + DEPTH * C + 1)
                    for k in range(TPC):
                        last = te.matmul(ps_w[b % 2][:, k * W:(k + 1) * W], h3[b % 2][:, k * P:(k + 1) * P], l3w2_sb[:, :],
                                         start=True, stop=True)
                    last.then_inc(w_ready, 1)

                pe.wait_ge(xs_ready, p)
                if p == 1:
                    pipeline(pe, [(first, 0), (second, 1), (weights, 2), (tile_sums, 4), (gather_of(p), 0)], lead=8)
                elif p < L2:
                    pipeline(pe, [(weights, 1), (tile_sums, 3), (gather_of(p), 0)])
                elif p < L3:
                    pipeline(pe, [(tile_sums, 3), (gather_of(p), 0)])
                else:
                    pe.wait_ge(bias_rows, 1)
                    pipeline(pe, [(hidden3, 0), (weights3, 1), (gather_of(p), 0), (tile_sums, 3)])
                w = F + 1 if p == 1 else F
                pe.wait_ge(lmv_ready, p)
                for t in range(LT):
                    last = te.matmul(ps_agg[:, 0:HI * w], l_lo[:, t, :], lmv[:, t * HI * w:(t + 1) * HI * w],
                                     start=(t == 0), stop=(t == LT - 1))
                last.then_inc(agg_ready, 1)
                if p < L2:
                    dense(W_ROOT + p - 1)
                elif p == L2:
                    dense(W_1A)
                    dense(W_1B)
                elif p == L2 + 1:
                    dense(W_2A)
                    dense(W_2B)
                else:
                    for k in range(2):
                        pe.wait_ge(col_in, k + 1)
                        te.matmul(ps_o[:, 0:NF], ones[:, :], t1[:, 0:NF], start=True, stop=True).then_inc(col_out, 1)

        @block.vector
        def _(dve):
            dve.sem_inc(w_free, 2)

            def linker(chain, base):
                n = [0]

                def done(op, wait=True):
                    n[0] += 1
                    op.then_inc(chain, 1)
                    if wait:
                        dve.wait_ge(chain, base + n[0])
                return done

            done = linker(setup_chain, 0)
            v.memset(xn[:, :], 0.0).then_inc(consts_made, 1)
            done(v.memset(zer[:, :], 0.0), False)
            done(v.memset(nodes[:, :], 0.0), False)
            done(v.memset(ones[:, :], 1.0), False)
            done(v.memset(kb3_rows[:, :], 0.0), False)
            done(v.memset(ones_rows[:, :], 0.0), False)
            done(v.memset(st[:, :, :], 0.0))
            dve.wait_ge(loaded, 16 * (N_LOADS + 1))
            done(v.tensor_copy(kb3_h, kb3_f))
            done(v.tensor_tensor(kb3_r, kb3_f, kb3_h, ALU.subtract))
            done(v.tensor_copy(kb3_m, kb3_r))
            done(v.tensor_tensor(kb3_r, kb3_r, kb3_m, ALU.subtract))
            for row, part in ((0, kb3_h), (32, kb3_m), (64, kb3_r)):
                done(v.tensor_copy(kb3_rows[row:row + 1, :], part[row:row + 1, :]))
                done(v.memset(ones_rows[row:row + 1, :], 1.0))

            def split(parts, whole):
                done(v.tensor_copy(parts[0], whole))
                done(v.tensor_tensor(whole, whole, parts[0], ALU.subtract))
                done(v.tensor_copy(parts[1], whole))
                done(v.tensor_tensor(parts[2], whole, parts[1], ALU.subtract))

            w_parts = [w1_p[:, k, :] for k in range(3)]
            split(w_parts, w1_f[:, :])
            for k in range(3):
                done(v.tensor_scalar(w_parts[k], w_parts[k], part_row[k], None, ALU.mult))
            done(v.tensor_tensor(w_parts[0], w_parts[0], w_parts[1], ALU.add))
            done(v.tensor_tensor(w1_sb[:, :], w_parts[0], w_parts[2], ALU.add))
            dve.sem_inc(consts_made, 1)
            dve.wait_ge(edges_loaded, 16 * 9)
            done(v.tensor_tensor(start, row_i, nxr_i, ALU.not_equal))
            v.tensor_scalar(start, start, NEG, None, ALU.mult).then_inc(start_made, 1)
            v.tensor_scalar(drow_h, row_i, -2048.0, None, ALU.add).then_inc(start_made, 1)
            done(v.tensor_scalar(tmp_i, src_i, 10, 7, ALU.arith_shift_right, ALU.logical_shift_left))
            done(v.tensor_scalar(src_i, src_i, P - 1, None, ALU.bitwise_and))
            v.tensor_tensor(key_h, tmp_i, src_i, ALU.add).then_inc(start_made, 1)
            done(v.tensor_tensor(end_f, dst_i, nxt_i, ALU.not_equal))
            done(v.tensor_scalar(end_f, end_f, -float(FAR), float(FAR), ALU.mult, ALU.add))
            done(v.tensor_tensor(end_row[:, :], end_f, dst_i, ALU.add))
            done(v.tensor_scalar(dcol[:, :], dst_i, -2048.0, None, ALU.add))
            done(v.memset(msg[:, :, :, :], 1.0))
            dve.wait_ge(start_stored, 16 * 3)
            done(v.memset(mm[:, :, 0:1], NEG))
            for q in range(2):
                done(v.memset(e16[q], 0.0))
            dve.sem_inc(setup_done, 1)

            def front(c, b, r):
                q = b % 2
                dve.wait_ge(a_wa, c + 1)
                dve.wait_ge(a_xr, c + 1)
                if started(c, 1):
                    dve.wait_ge(a_d, c)
                v.tensor_tensor(e2, ps_wa, xr[q], ALU.mult).then_inc(a_e2, 1)
                dve.wait_ge(a_neg[q], turn(b, r) * 16 + 16)
                if started(c, 1):
                    dve.wait_ge(a_carry, c)
                dve.wait_ge(a_e2, c + 1)
                for h in range(2):
                    last = v.tensor_tensor_scan(mm[:, h, 1:CH + 1], e2[:, h * CH:(h + 1) * CH], neg[q],
                                                mm[:, h, 0:1], ALU.max, ALU.add)
                last.then_inc(a_m, 1)
                dve.wait_ge(a_wm, c + 1)
                v.tensor_tensor(e1[q], ps_wm, xr[q], ALU.mult).then_inc(a_e1, 1)
                dve.wait_ge(a_m, c + 1)
                if started(c, 2):
                    dve.wait_ge(a_ab, c - 1)
                v.tensor_tensor(dd[q].rearrange("p (h n) -> p h n", h=2), mm[:, :, 0:CH],
                                e2.rearrange("p (h n) -> p h n", h=2), ALU.subtract).then_inc(a_d, 1)
                dve.wait_ge(a_d, c + 1)
                v.tensor_copy(mm[:, :, 0:1], mm[:, :, CH:CH + 1]).then_inc(a_carry, 1)

            def sums(c, b, r):
                q = b % 2
                dve.wait_ge(a_ab, c + 1)
                if started(c, 1):
                    dve.wait_ge(a_q, c)
                v.tensor_tensor(be, bb[q], e1[q], ALU.mult).then_inc(a_be, 1)
                if started(c, 2):
                    dve.wait_ge(a_t, (c - 1) * TPC)
                for dst_ap, src_ap in ((ss, bb[q]), (qq, be)):
                    for h in range(2):
                        at = slice(h * CH, (h + 1) * CH)
                        before = dst_ap[1 - q][:, (h + 1) * CH - 1:(h + 1) * CH] if started(c, 1) else 0.0
                        last = v.tensor_tensor_scan(dst_ap[q][:, at], aa[q][:, at], src_ap[:, at], before, ALU.mult, ALU.add)
                    if dst_ap is ss:
                        dve.wait_ge(a_be, c + 1)
                last.then_inc(a_q, 1)

            pipeline(dve, [(front, 0), (sums, 1)])

            done = linker(node_chain, 0)
            n_z = n_fn = n_col = 0

            def blocks(ap):
                return ap.rearrange("p (h f) -> p h f", f=F)

            def over_f(ap):
                return ap.unsqueeze(2).broadcast_to([P, HI, F])

            def over_h(ap):
                return ap.unsqueeze(1).broadcast_to([P, HI, F])

            N1, N2, ND = blocks(t1[:, 0:NF]), blocks(t2[:, 0:NF]), blocks(nodes[:, 0:NF])
            XN, DENSE = blocks(xn[:, 0:NF]), blocks(ps_o[:, 0:NF])

            def function():
                nonlocal n_fn
                n_fn += 1
                dve.sem_inc(act_in, 1)
                dve.wait_ge(act_out, n_fn)

            def dense():
                nonlocal n_z
                n_z += 1
                dve.sem_inc(z_ready, 1)
                dve.wait_ge(dense_ready, n_z)

            def layernorm():
                done(v.tensor_reduce(st[:, 0, :], N1, X, ALU.add))
                done(v.tensor_scalar(st[:, 1, :], st[:, 0, :], 1.0 / F, None, ALU.mult))
                done(v.tensor_tensor(N1, N1, over_f(st[:, 1, :]), ALU.subtract))
                done(v.tensor_tensor(N2, N1, N1, ALU.mult))
                done(v.tensor_reduce(st[:, 0, :], N2, X, ALU.add))
                done(v.tensor_scalar(st[:, 2, :], st[:, 0, :], 1.0 / F, LN_EPS, ALU.mult, ALU.add))
                function()
                done(v.reciprocal(st[:, 4, :], st[:, 3, :]))
                done(v.tensor_tensor(ND, N1, over_f(st[:, 4, :]), ALU.mult))
                done(v.tensor_copy(xn[:, 0:NF], nodes[:, 0:NF]))

            dve.wait_ge(ef_loaded, 16)
            split(ef_p, ef_f)
            dve.sem_inc(ef_made, 1)
            for k in range(SPLIT):
                dve.wait_ge(sums_loaded[k], 16)
                at = slice(k * HI // SPLIT, (k + 1) * HI // SPLIT)
                den, num = sq[:, at, 0:W], sq[:, at, W:2 * W]
                done(v.tensor_scalar(den, den, 1.0, None, ALU.max))
                done(v.reciprocal(den, den))
                done(v.tensor_tensor(num, num, den, ALU.mult))
                done(v.tensor_reduce(N2[:, at, :], num.rearrange("p h (i o) -> p h o i", i=F), X, ALU.add))
            done(v.tensor_tensor(N1, N2, XN, ALU.add))
            layernorm()
            e_of = sq[:, :, 2 * W:SW].rearrange("p h o -> p (h o)")
            done(v.tensor_scalar(st[:, 0, :], e_of, 0.0, float(EP + 1), ALU.is_equal, ALU.mult))
            done(v.tensor_scalar(st[:, 1, :], e_of, -1.0, None, ALU.add))
            done(v.tensor_tensor(last_row[:, :], st[:, 0, :], st[:, 1, :], ALU.add))
            dve.wait_ge(ef_stored, 16 * 3)
            done(v.tensor_scalar(s_i, src_sb[:, :], 7, GROUP - 1, ALU.logical_shift_right, ALU.bitwise_and))
            done(v.tensor_copy(s_f, s_i))
            done(v.tensor_tensor(sel8, iota[:, 0:GROUP].unsqueeze(1).broadcast_to([P, T, GROUP]),
                                 s_f.unsqueeze(2).broadcast_to([P, T, GROUP]), ALU.is_equal))
            iota_l = iota[0:CB, :].unsqueeze(1).broadcast_to([CB, LT, P])
            done(v.tensor_tensor(l_f[:, 0, :], last_sb[:, 0, :], last_sb[:, 1, :], ALU.is_equal))
            done(v.tensor_scalar(l_i, last_sb[:, 0, :], P - 1, None, ALU.bitwise_and))
            done(v.tensor_copy(l_f[:, 1, :], l_i))
            done(v.tensor_scalar(l_i, last_sb[:, 0, :], 7, None, ALU.logical_shift_right))
            done(v.tensor_scalar(l_f[:, 2, :], l_i, 1.0, None, ALU.add))
            done(v.tensor_tensor(l_f[:, 3, :], l_f[:, 2, :], l_f[:, 0, :], ALU.mult))
            done(v.tensor_scalar(l_f[:, 2, :], l_f[:, 3, :], -1.0, None, ALU.add))
            done(v.tensor_tensor(l_lo, iota_l, l_f[:, 1, :].unsqueeze(2).broadcast_to([CB, LT, P]), ALU.is_equal))
            done(v.tensor_tensor(l_hi, iota_l[:, :, 0:HI], l_f[:, 2, :].unsqueeze(2).broadcast_to([CB, LT, HI]), ALU.is_equal))
            dve.sem_inc(nodes_ready, 1)

            for p in range(1, PHASES):
                if p == L3:
                    for q in range(2):
                        done(v.memset(h3[q][EH:P, :], 0.0))
                        done(v.memset(h3[q][EH:EH + 1, :], 1.0))
                    dve.sem_inc(bias_rows, 1)
                wp = p - 1 if p < L2 else DEPTH

                done(v.tensor_copy(xs_r, nodes[:, :]))
                split(xs, xs_r)
                dve.sem_inc(xs_ready, 1)

                def hots(c, b, r, p=p):
                    if b not in by_pe(p):
                        return
                    q, n = b // 2, nth(by_pe(p), b, r) + GB[p]
                    dve.wait_ge(key_loaded[q], (r + KB[p][q] + 1) * 16)
                    if started(c, 4) or GB[p]:
                        dve.wait_ge(picks_ready, n + 1 - len(by_pe(p)))
                    at = slice(first_by_pe(p) * P, CH)
                    for j in range(NG):
                        last = v.tensor_scalar(hot[q][:, j, at], keys[q][:, at], key_of[:, j:j + 1], None, ALU.is_equal)
                    last.then_inc(hot_ready, 1)

                def message(c, b, r, p=p, wp=wp):
                    q, at = b % 2, c + (p - 1) * C
                    plain = p in (L2, L2 + 1)
                    x_rows = xg[:, b, :].rearrange("p (k f) -> p k f", f=F)
                    k0 = first_by_pe(p)
                    if b in by_pe(p):
                        n = nth(by_pe(p), b, r) + GB[p]
                        dve.wait_ge(picks_ready, n + 1)
                        if started(c, 4) or GB[p] or b != by_pe(p)[0]:
                            dve.wait_ge(pick_done, n)
                        if plain and started(c, 4):
                            dve.wait_ge(y_ready, at - 3)
                        pk = picked[:, k0 * P:CH].rearrange("p (k h f) -> p k h f", h=GROUP, f=F)
                        v.tensor_tensor(pk, ps_g(p, b)[:, k0 * P:CH].rearrange("p (k h f) -> p k h f", h=GROUP, f=F),
                                        sel8[:, bass.ds(c * TPC + k0, TPC - k0), :].unsqueeze(3)
                                        .broadcast_to([P, TPC - k0, GROUP, F]), ALU.mult).then_inc(picked_ready, 1)
                    if not plain:
                        dve.wait_ge(xg_loaded[b], rows_in(p, b, r))
                    def compare():
                        if started(c, 2):
                            dve.wait_ge(y_ready, at - 1)
                        dve.wait_ge(drow_loaded[b // 2], (r + (p - 1) * (C // 4) + 1) * 16)
                        for k in range(TPC):
                            o = q * CH + k * P
                            last = v.tensor_scalar(same[q][:, k, :], drow[b // 2][:, o:o + P],
                                                   dcol[:, bass.ds(c * TPC + k, 1)], None, ALU.is_equal)
                        return last

                    if b in by_pe(p):
                        dve.wait_ge(picked_ready, n + 1)
                        v.tensor_reduce(x_rows[:, k0:TPC, :], pk.rearrange("p k h f -> p k f h"), X, ALU.add).then_inc(pick_done, 1)
                        if plain:
                            dve.wait_ge(pick_done, n + 1)
                    if plain:
                        compare().then_inc(msg_ready, 1)
                        return
                    if b in by_pe(p):
                        dve.wait_ge(pick_done, n + 1)
                    dve.wait_ge(w_ready, c + wp * C + 1)
                    v.tensor_tensor(prod.rearrange("p (k i o) -> p k i o", i=F, o=F),
                                    ps_w[q].rearrange("p (k i o) -> p k i o", i=F, o=F),
                                    x_rows.unsqueeze(3).broadcast_to([P, TPC, F, F]), ALU.mult).then_inc(w_free, 1)
                    compare()
                    dve.wait_ge(w_free, c + wp * C + 3)
                    v.tensor_reduce(msg[:, q, :, 0:F], prod.rearrange("p (k i o) -> p k o i", i=F, o=F), X, ALU.add)\
                     .then_inc(msg_ready, 1)
                    dve.wait_ge(msg_ready, at + 1)

                pipeline(dve, [(hots, 0), (message, 3)])
                w = F + 1 if p == 1 else F
                dve.wait_ge(last_loaded, 32 * p)
                v.tensor_tensor(lmv[:, 0:LT * HI * w].rearrange("p (t h f) -> p t h f", t=LT, f=w),
                                lrow[:, 0:LT * w].rearrange("p (t f) -> p t f", f=w).unsqueeze(2).broadcast_to([CB, LT, HI, w]),
                                l_hi.unsqueeze(3).broadcast_to([CB, LT, HI, w]), ALU.mult).then_inc(lmv_ready, 1)
                dve.wait_ge(agg_ready, p)
                dve.wait_ge(yg_loaded, 16 * HI * p)
                done(v.tensor_tensor(agg[:, 0:HI * w], yg[:, 0:HI * w], ps_agg[:, 0:HI * w], ALU.add))
                AGG = agg[:, 0:HI * w].rearrange("p (h f) -> p h f", f=w)[:, :, 0:F]
                if p == 1:
                    deg = agg[:, 0:HI * w].rearrange("p (h f) -> p h f", f=w)[:, :, F:w].rearrange("p h o -> p (h o)")
                    done(v.tensor_scalar(st[:, 0, :], deg, 1.0, None, ALU.max))
                    done(v.reciprocal(inv_deg1[:, :], st[:, 0, :]))
                    done(v.tensor_scalar(st[:, 1, :], deg, 0.0, None, ALU.is_gt))
                    done(v.tensor_tensor(inv_deg[:, :], st[:, 1, :], inv_deg1[:, :], ALU.mult))
                if p < L2:
                    done(v.tensor_tensor(N1, AGG, over_f(inv_deg[:, :]), ALU.mult))
                    dense()
                    done(v.tensor_tensor(N1, N1, DENSE, ALU.add))
                    done(v.tensor_tensor(N1, N1, over_h(nb[:, B_ROOT + p - 1, :]), ALU.add))
                    function()
                    if p == L2 - 1:
                        done(v.tensor_tensor(N1, XN, ND, ALU.add))
                        layernorm()
                elif p < L3:
                    q = p - L2
                    done(v.tensor_scalar(st[:, 0, 0:1], eps_sb[:, q:q + 1], 1.0, None, ALU.add))
                    done(v.tensor_scalar(t1[:, 0:NF], nodes[:, 0:NF], st[:, 0, 0:1], None, ALU.mult))
                    done(v.tensor_tensor(ND, N1, AGG, ALU.add))
                    dense()
                    done(v.tensor_tensor(N1, DENSE, over_h(nb[:, B_1A + 2 * q, :]), ALU.add))
                    done(v.tensor_scalar(nodes[:, 0:NF], t1[:, 0:NF], 0.0, None, ALU.max))
                    dense()
                    done(v.tensor_tensor(N1, DENSE, over_h(nb[:, B_1B + 2 * q, :]), ALU.add))
                    if q == 0:
                        done(v.tensor_scalar(nodes[:, 0:NF], t1[:, 0:NF], 0.0, None, ALU.max))
                    else:
                        done(v.tensor_reduce(st[:, 0, :], N1, X, ALU.max))
                        done(v.tensor_tensor(N1, N1, over_f(st[:, 0, :]), ALU.subtract))
                        function()
                        done(v.tensor_reduce(st[:, 2, :], N2, X, ALU.add))
                        function()
                        done(v.tensor_tensor(N1, N1, over_f(st[:, 3, :]), ALU.subtract))
                        done(v.tensor_tensor(N1, N1, XN, ALU.add))
                        layernorm()
                else:
                    done(v.tensor_tensor(N1, AGG, over_f(inv_deg1[:, :]), ALU.mult))
                    done(v.tensor_tensor(N1, N1, over_h(nb[:, B_BIAS, :]), ALU.add))
                    done(v.tensor_scalar(t1[:, 0:NF], t1[:, 0:NF], 0.0, None, ALU.max))
                    done(v.tensor_tensor(N1, N1, over_f(valid), ALU.mult))
                    for k in range(2):
                        dve.sem_inc(col_in, 1)
                        dve.wait_ge(col_out, k + 1)
                        done(v.tensor_reduce(fs[:, 0, :], ps_o[:, 0:NF].rearrange("p (h f) -> p f h", f=F), X, ALU.add))
                        if k == 0:
                            done(v.tensor_scalar(fs[:, 1, :], fs[:, 0, :], 1.0 / N, None, ALU.mult))
                            done(v.tensor_tensor(ND, N1, over_h(fs[:, 1, :]), ALU.subtract))
                            done(v.tensor_tensor(N2, ND, over_f(valid), ALU.mult))
                            done(v.tensor_tensor(N1, N2, N2, ALU.mult))
                    done(v.tensor_scalar(fs[:, 2, :], fs[:, 0, :], 1.0 / N, BN_EPS, ALU.mult, ALU.add))
                    function()
                    done(v.reciprocal(fs[:, 1, :], fs[:, 3, :]))
                    done(v.tensor_tensor(fs[:, 0, :], fs[:, 1, :], nb[:, B_GAMMA, :], ALU.mult))
                    done(v.tensor_tensor(N1, ND, over_h(fs[:, 0, :]), ALU.mult))
                    done(v.tensor_tensor(N1, N1, over_h(nb[:, B_BETA, :]), ALU.add))
                    done(v.tensor_tensor(N1, N1, XN, ALU.add))
                    layernorm()
                dve.sem_inc(nodes_ready, 1)


_OUT = ((N, F), 'float32')


def kernel(**inputs):
    import numpy as np
    import concourse.bacc as bacc
    from concourse.bass_utils import run_bass_kernel_spmd as run

    a = {k: np.asarray(val) for k, val in inputs.items()}

    def tiles(row):
        return np.ascontiguousarray(row.reshape(T, P).T)

    def with_bias(w, b):
        return np.concatenate([w, b[None, :]], axis=0)

    def full(w):
        o = np.zeros((P, W), np.float32)
        o[:len(w)] = w
        return o

    def padded(attr):
        d = attr.shape[1]
        o = np.zeros((d + 1, EP), np.float32)
        o[:d, :E] = attr.T
        o[d] = 1.0
        return o

    src = np.zeros(EP, np.int32)
    src[:E] = a['src']
    dst = np.full(EP, NPAD, np.int32)
    dst[:E] = a['dst']
    nxt = np.full(EP, -1, np.int32)
    nxt[:-1] = dst[1:]

    rows_of = np.arange(1, EP + 1, dtype=np.float32).reshape(C, P, TPC)
    edge_no = np.ascontiguousarray(rows_of.transpose(1, 0, 2).reshape(P, T))
    by_chunk = np.stack([dst[P - 1::P], nxt[P - 1::P]]).reshape(2, 2, CB, TPC).transpose(0, 2, 1, 3).reshape(2, CB, LT)

    mats = list(a['L1_gnn_root_W']) + [a[f'L2_gnn_{k}'] for k in ('w1a', 'w1b', 'w2a', 'w2b')]
    node_w = np.zeros((P, NWM, P), np.float32)
    for n, m in enumerate(mats):
        for q in range(P // F):
            node_w[q * F:(q + 1) * F, n, q * F:(q + 1) * F] = m
    rows = list(a['L1_gnn_root_b']) + [a[f'L2_gnn_{k}'] for k in ('b1a', 'b1b', 'b2a', 'b2b')] + \
        [a[f'L3_gnn_{k}'] for k in ('bias', 'gamma', 'beta')]
    node_b = np.ascontiguousarray(np.broadcast_to(np.stack(rows), (P, NBR, F)))
    eps = np.ascontiguousarray(np.broadcast_to(np.stack([a['L2_gnn_eps1'], a['L2_gnn_eps2']]), (P, 2)))

    consts = np.zeros((P, NK), np.float32)
    consts[:, K_ID:K_ID + P] = np.eye(P)
    consts[:, K_IOTA:K_IOTA + P] = np.arange(P)
    consts[:, K_KEY:K_KEY + NG] = np.arange(P)[:, None] + P * np.arange(NG)[None, :]
    for k in range(3):
        consts[k * (R6 // 3):(k + 1) * (R6 // 3), K_PART + k] = 1.0
    consts[:, K_VALID:K_VALID + HI] = (np.arange(HI)[None, :] * P + np.arange(P)[:, None]) < N

    data = {
        'x': a['x'], 'src_t': tiles(src), 'dst_t': tiles(dst), 'dst_next_t': tiles(nxt),
        'dst_row': dst.reshape(P, T), 'dst_next_row': nxt.reshape(P, T), 'src_row': src.reshape(P, T),
        'dst_last': by_chunk[0], 'dst_after': by_chunk[1], 'edge_no': edge_no,
        'ef16': padded(a['edge_attr_16']), 'ef6': padded(a['edge_attr_6']),
        'w_attn': full(with_bias(a['L0_gnn_W_attn'], a['L0_gnn_b_attn'])),
        'w_msg': full(with_bias(a['L0_gnn_W_msg'], a['L0_gnn_b_msg'])),
        'w1': np.tile(np.concatenate([with_bias(a['L1_gnn_kW1'], a['L1_gnn_kb1']),
                                      with_bias(a['L3_gnn_W1'], a['L3_gnn_b1']), np.zeros((D6 + 1, KD - EH), np.float32)],
                                     axis=1), (9, 1)),
        'kw2': a['L1_gnn_kW2'], 'kb2': a['L1_gnn_kb2'].reshape(KD, 1),
        'kw3': a['L1_gnn_kW3'], 'kb3': a['L1_gnn_kb3'],
        'l3w2': full(with_bias(a['L3_gnn_W2'], a['L3_gnn_b2'])),
        'node_w': node_w, 'node_b': node_b, 'eps': eps, 'consts': consts,
    }
    nc = bacc.Bacc("TRN2", target_bir_lowering=False, num_devices=1)
    arrays, args = {}, []
    for name, val in data.items():
        val = np.ascontiguousarray(val)
        arrays[f"in_{name}"] = val
        args.append(nc.dram_tensor(f"in_{name}", val.shape, mybir.dt.from_np(val.dtype), kind="ExternalInput").ap())
    out = nc.dram_tensor("out_nodes", _OUT[0], mybir.dt.from_np(np.dtype(_OUT[1])), kind="ExternalOutput").ap()
    gnn_resnorm(nc, *args, out)
    r = run(nc, [arrays], core_ids=[0])
    return r.results[0]["out_nodes"]
```
